# Optimizing a Trainium2 kernel written in Bass

```python
import numpy as np
import jax
import jax.numpy as jnp

def _softmax(x, axis=-1):
    return jax.nn.softmax(x, axis=axis)

def _gelu(x):
    return jax.nn.gelu(x, approximate=True)

def _silu(x):
    return jax.nn.silu(x)

def _sigmoid(x):
    return jax.nn.sigmoid(x)

def _layernorm(x, axis=-1, eps=1e-05):
    m = jnp.mean(x, axis=axis, keepdims=True)
    v = jnp.var(x, axis=axis, keepdims=True)
    return (x - m) / jnp.sqrt(v + eps)

def _scatter_add(tgt, idx, src, axis=0):
    return tgt.at[idx].add(src)

def _segment_sum(src, seg, n):
    return jax.ops.segment_sum(src, seg, n)
kernel_name = 'mk_seq_postln_d2_jaxref_r8_5c4605'

def setup_inputs(seed: int=0):
    np.random.seed(seed)
    _w = jnp.asarray

    def _L0_attn_setup():
        import math
        import jax, jax.numpy as jnp
        import numpy as np
        L, D, H, F = (4, 128, 16, 512)
        HD = D // H
        EPS = 1e-05

        def get_alibi_slopes(num_heads):
            closest = 2 ** math.floor(math.log2(num_heads))
            base = 2 ** (-2 ** (-(math.log2(closest) - 3)))
            slopes = base ** np.arange(1, closest + 1)
            if closest != num_heads:
                extra_base = 2 ** (-2 ** (-(math.log2(2 * closest) - 3)))
                extra = extra_base ** np.arange(1, 2 * (num_heads - closest) + 1, 2)
                slopes = np.concatenate([slopes, extra])
            return jnp.asarray(slopes, dtype=jnp.float32)

        def build_mask(num_heads, T):
            pos = jnp.arange(T)
            dist = pos[None, :] - pos[:, None]
            alibi = get_alibi_slopes(num_heads)[:, None, None] * dist[None]
            causal = jnp.where(dist > 0, -jnp.inf, 0.0).astype(jnp.float32)
            return causal[None] + alibi

        def layer_norm(x, w, b):
            mu = jnp.mean(x, axis=-1, keepdims=True)
            var = jnp.mean(jnp.square(x - mu), axis=-1, keepdims=True)
            return (x - mu) * jax.lax.rsqrt(var + EPS) * w + b

        def mha(x, mask, Wi, bi, Wo, bo):
            B, T, _ = x.shape
            qkv = x @ Wi.T + bi
            q, k, v = jnp.split(qkv, 3, axis=-1)
            q = q.reshape(B, T, H, HD).transpose(0, 2, 1, 3)
            k = k.reshape(B, T, H, HD).transpose(0, 2, 1, 3)
            v = v.reshape(B, T, H, HD).transpose(0, 2, 1, 3)
            scores = jnp.einsum('bhqd,bhkd->bhqk', q, k) / math.sqrt(HD)
            scores = scores + mask[None]
            attn = jax.nn.softmax(scores, axis=-1)
            out = jnp.einsum('bhqk,bhkd->bhqd', attn, v)
            out = out.transpose(0, 2, 1, 3).reshape(B, T, D)
            return out @ Wo.T + bo
        key = jax.random.key(seed)
        ks = jax.random.split(key, 13)
        s = 0.02
        inp = {'x': jax.random.normal(ks[0], (2, 256, D), dtype=jnp.float32), 'in_proj_w': jax.random.normal(ks[1], (L, 3 * D, D), dtype=jnp.float32) * s, 'in_proj_b': jnp.zeros((L, 3 * D), dtype=jnp.float32), 'out_proj_w': jax.random.normal(ks[2], (L, D, D), dtype=jnp.float32) * s, 'out_proj_b': jnp.zeros((L, D), dtype=jnp.float32), 'ffn1_w': jax.random.normal(ks[3], (L, F, D), dtype=jnp.float32) * s, 'ffn1_b': jnp.zeros((L, F), dtype=jnp.float32), 'ffn2_w': jax.random.normal(ks[4], (L, D, F), dtype=jnp.float32) * s, 'ffn2_b': jnp.zeros((L, D), dtype=jnp.float32), 'ln1_w': jnp.ones((L, D), dtype=jnp.float32), 'ln1_b': jnp.zeros((L, D), dtype=jnp.float32), 'ln2_w': jnp.ones((L, D), dtype=jnp.float32), 'ln2_b': jnp.zeros((L, D), dtype=jnp.float32), 'final_w': jnp.ones((D,), dtype=jnp.float32), 'final_b': jnp.zeros((D,), dtype=jnp.float32)}
        return inp
    _L0_attn_in = _L0_attn_setup()

    def _L0_ffn_setup():
        import jax, jax.numpy as jnp
        import numpy as np
        D_IN, D_HID = (128, 512)

        def _ternary(key, shape):
            return jax.random.randint(key, shape, -1, 2).astype(jnp.float32)

        def _tlin(x, w, s):
            return jnp.einsum('bsi,oi->bso', x, w) * s
        key = jax.random.key(seed)
        ks = jax.random.split(key, 12)
        inv = lambda fan: 1.0 / np.sqrt(fan).astype(np.float32)
        return {'x': jax.random.normal(ks[0], (4, 256, D_IN), dtype=jnp.float32), 'w1_w': _ternary(ks[1], (D_HID, D_IN)), 'w1_s': jax.random.uniform(ks[2], (D_HID,), dtype=jnp.float32) * inv(D_IN), 'w2_w': _ternary(ks[3], (D_HID, D_IN)), 'w2_s': jax.random.uniform(ks[4], (D_HID,), dtype=jnp.float32) * inv(D_IN), 'h1_w': _ternary(ks[5], (D_HID, D_HID)), 'h1_s': jax.random.uniform(ks[6], (D_HID,), dtype=jnp.float32) * inv(D_HID), 'h2_w': _ternary(ks[7], (D_HID, D_HID)), 'h2_s': jax.random.uniform(ks[8], (D_HID,), dtype=jnp.float32) * inv(D_HID), 'w3_w': _ternary(ks[9], (D_IN, D_HID)), 'w3_s': jax.random.uniform(ks[10], (D_IN,), dtype=jnp.float32) * inv(D_HID)}
    _L0_ffn_in = _L0_ffn_setup()

    def _L1_attn_setup():
        import jax, jax.numpy as jnp
        import numpy as np
        EMBED_DIM = 128
        NUM_HEADS = 16
        EFF_HEADS = NUM_HEADS // 2
        HEAD_DIM = EMBED_DIM // NUM_HEADS
        LAMBDA_INIT = 0.8
        B, N = (2, 256)
        key = jax.random.key(seed)
        ks = jax.random.split(key, 14)
        s = 0.02
        return {'x': jax.random.normal(ks[0], (B, N, EMBED_DIM), dtype=jnp.float32), 'Wq': jax.random.normal(ks[1], (EMBED_DIM, EMBED_DIM), dtype=jnp.float32) * s, 'bq': jnp.zeros((EMBED_DIM,), dtype=jnp.float32), 'Wk': jax.random.normal(ks[2], (EMBED_DIM, EMBED_DIM), dtype=jnp.float32) * s, 'bk': jnp.zeros((EMBED_DIM,), dtype=jnp.float32), 'Wv': jax.random.normal(ks[3], (EMBED_DIM, EMBED_DIM), dtype=jnp.float32) * s, 'bv': jnp.zeros((EMBED_DIM,), dtype=jnp.float32), 'Wp': jax.random.normal(ks[4], (EMBED_DIM, EMBED_DIM), dtype=jnp.float32) * s, 'bp': jnp.zeros((EMBED_DIM,), dtype=jnp.float32), 'lambda_q1': jax.random.normal(ks[5], (EFF_HEADS, 1, HEAD_DIM), dtype=jnp.float32) * s, 'lambda_k1': jax.random.normal(ks[6], (EFF_HEADS, 1, HEAD_DIM), dtype=jnp.float32) * s, 'lambda_q2': jax.random.normal(ks[7], (EFF_HEADS, 1, HEAD_DIM), dtype=jnp.float32) * s, 'lambda_k2': jax.random.normal(ks[8], (EFF_HEADS, 1, HEAD_DIM), dtype=jnp.float32) * s}
    _L1_attn_in = _L1_attn_setup()

    def _L1_ffn_setup():
        import jax, jax.numpy as jnp
        import numpy as np
        B, S, D = (4, 256, 128)
        E, F = (8, 512)
        key = jax.random.key(seed)
        ks = jax.random.split(key, 5)
        x = jax.random.normal(ks[0], (B, S, D), dtype=jnp.float32)
        switch_w = jax.random.normal(ks[1], (D, E), dtype=jnp.float32) * D ** (-0.5)
        switch_b = jnp.zeros((E,), dtype=jnp.float32)
        w1 = jax.random.normal(ks[2], (E, D, F), dtype=jnp.float32) * D ** (-0.5)
        b1 = jnp.zeros((E, F), dtype=jnp.float32)
        w2 = jax.random.normal(ks[3], (E, F, D), dtype=jnp.float32) * F ** (-0.5)
        b2 = jnp.zeros((E, D), dtype=jnp.float32)
        return {'x': x, 'switch_w': switch_w, 'switch_b': switch_b, 'w1': w1, 'b1': b1, 'w2': w2, 'b2': b2}
    _L1_ffn_in = _L1_ffn_setup()
    _d = {'L0_attn_x': _L0_attn_in['x'], 'L0_attn_in_proj_w': _L0_attn_in['in_proj_w'], 'L0_attn_in_proj_b': _L0_attn_in['in_proj_b'], 'L0_attn_out_proj_w': _L0_attn_in['out_proj_w'], 'L0_attn_out_proj_b': _L0_attn_in['out_proj_b'], 'L0_attn_ffn1_w': _L0_attn_in['ffn1_w'], 'L0_attn_ffn1_b': _L0_attn_in['ffn1_b'], 'L0_attn_ffn2_w': _L0_attn_in['ffn2_w'], 'L0_attn_ffn2_b': _L0_attn_in['ffn2_b'], 'L0_attn_ln1_w': _L0_attn_in['ln1_w'], 'L0_attn_ln1_b': _L0_attn_in['ln1_b'], 'L0_attn_ln2_w': _L0_attn_in['ln2_w'], 'L0_attn_ln2_b': _L0_attn_in['ln2_b'], 'L0_attn_final_w': _L0_attn_in['final_w'], 'L0_attn_final_b': _L0_attn_in['final_b'], 'L0_ffn_w1_w': _L0_ffn_in['w1_w'], 'L0_ffn_w1_s': _L0_ffn_in['w1_s'], 'L0_ffn_w2_w': _L0_ffn_in['w2_w'], 'L0_ffn_w2_s': _L0_ffn_in['w2_s'], 'L0_ffn_h1_w': _L0_ffn_in['h1_w'], 'L0_ffn_h1_s': _L0_ffn_in['h1_s'], 'L0_ffn_h2_w': _L0_ffn_in['h2_w'], 'L0_ffn_h2_s': _L0_ffn_in['h2_s'], 'L0_ffn_w3_w': _L0_ffn_in['w3_w'], 'L0_ffn_w3_s': _L0_ffn_in['w3_s'], 'L1_attn_Wq': _L1_attn_in['Wq'], 'L1_attn_bq': _L1_attn_in['bq'], 'L1_attn_Wk': _L1_attn_in['Wk'], 'L1_attn_bk': _L1_attn_in['bk'], 'L1_attn_Wv': _L1_attn_in['Wv'], 'L1_attn_bv': _L1_attn_in['bv'], 'L1_attn_Wp': _L1_attn_in['Wp'], 'L1_attn_bp': _L1_attn_in['bp'], 'L1_attn_lambda_q1': _L1_attn_in['lambda_q1'], 'L1_attn_lambda_k1': _L1_attn_in['lambda_k1'], 'L1_attn_lambda_q2': _L1_attn_in['lambda_q2'], 'L1_attn_lambda_k2': _L1_attn_in['lambda_k2'], 'L1_ffn_switch_w': _L1_ffn_in['switch_w'], 'L1_ffn_switch_b': _L1_ffn_in['switch_b'], 'L1_ffn_w1': _L1_ffn_in['w1'], 'L1_ffn_b1': _L1_ffn_in['b1'], 'L1_ffn_w2': _L1_ffn_in['w2'], 'L1_ffn_b2': _L1_ffn_in['b2']}
    _x0 = _d['L0_attn_x']
    _d['L0_attn_x'] = jax.random.normal(jax.random.fold_in(jax.random.key(seed), 1), (4, 1024, 128), dtype=_x0.dtype)
    del _x0
    return _d

def reference(L0_attn_x, L0_attn_in_proj_w, L0_attn_in_proj_b, L0_attn_out_proj_w, L0_attn_out_proj_b, L0_attn_ffn1_w, L0_attn_ffn1_b, L0_attn_ffn2_w, L0_attn_ffn2_b, L0_attn_ln1_w, L0_attn_ln1_b, L0_attn_ln2_w, L0_attn_ln2_b, L0_attn_final_w, L0_attn_final_b, L0_ffn_w1_w, L0_ffn_w1_s, L0_ffn_w2_w, L0_ffn_w2_s, L0_ffn_h1_w, L0_ffn_h1_s, L0_ffn_h2_w, L0_ffn_h2_s, L0_ffn_w3_w, L0_ffn_w3_s, L1_attn_Wq, L1_attn_bq, L1_attn_Wk, L1_attn_bk, L1_attn_Wv, L1_attn_bv, L1_attn_Wp, L1_attn_bp, L1_attn_lambda_q1, L1_attn_lambda_k1, L1_attn_lambda_q2, L1_attn_lambda_k2, L1_ffn_switch_w, L1_ffn_switch_b, L1_ffn_w1, L1_ffn_b1, L1_ffn_w2, L1_ffn_b2):

    def _L0_attn_ref(x, in_proj_w, in_proj_b, out_proj_w, out_proj_b, ffn1_w, ffn1_b, ffn2_w, ffn2_b, ln1_w, ln1_b, ln2_w, ln2_b, final_w, final_b):
        import math
        import jax, jax.numpy as jnp
        import numpy as np
        L, D, H, F = (4, 128, 16, 512)
        HD = D // H
        EPS = 1e-05

        def get_alibi_slopes(num_heads):
            closest = 2 ** math.floor(math.log2(num_heads))
            base = 2 ** (-2 ** (-(math.log2(closest) - 3)))
            slopes = base ** np.arange(1, closest + 1)
            if closest != num_heads:
                extra_base = 2 ** (-2 ** (-(math.log2(2 * closest) - 3)))
                extra = extra_base ** np.arange(1, 2 * (num_heads - closest) + 1, 2)
                slopes = np.concatenate([slopes, extra])
            return jnp.asarray(slopes, dtype=jnp.float32)

        def build_mask(num_heads, T):
            pos = jnp.arange(T)
            dist = pos[None, :] - pos[:, None]
            alibi = get_alibi_slopes(num_heads)[:, None, None] * dist[None]
            causal = jnp.where(dist > 0, -jnp.inf, 0.0).astype(jnp.float32)
            return causal[None] + alibi

        def layer_norm(x, w, b):
            mu = jnp.mean(x, axis=-1, keepdims=True)
            var = jnp.mean(jnp.square(x - mu), axis=-1, keepdims=True)
            return (x - mu) * jax.lax.rsqrt(var + EPS) * w + b

        def mha(x, mask, Wi, bi, Wo, bo):
            B, T, _ = x.shape
            qkv = x @ Wi.T + bi
            q, k, v = jnp.split(qkv, 3, axis=-1)
            q = q.reshape(B, T, H, HD).transpose(0, 2, 1, 3)
            k = k.reshape(B, T, H, HD).transpose(0, 2, 1, 3)
            v = v.reshape(B, T, H, HD).transpose(0, 2, 1, 3)
            scores = jnp.einsum('bhqd,bhkd->bhqk', q, k) / math.sqrt(HD)
            scores = scores + mask[None]
            attn = jax.nn.softmax(scores, axis=-1)
            out = jnp.einsum('bhqk,bhkd->bhqd', attn, v)
            out = out.transpose(0, 2, 1, 3).reshape(B, T, D)
            return out @ Wo.T + bo
        T = x.shape[1]
        mask = build_mask(H, T)
        for i in range(L):
            xn = layer_norm(x, ln1_w[i], ln1_b[i])
            x = x + mha(xn, mask, in_proj_w[i], in_proj_b[i], out_proj_w[i], out_proj_b[i])
            xn = layer_norm(x, ln2_w[i], ln2_b[i])
            h = jax.nn.gelu(xn @ ffn1_w[i].T + ffn1_b[i], approximate=False)
            x = x + (h @ ffn2_w[i].T + ffn2_b[i])
        return layer_norm(x, final_w, final_b)

    def _L0_ffn_ref(x, w1_w, w1_s, w2_w, w2_s, h1_w, h1_s, h2_w, h2_s, w3_w, w3_s):
        import jax, jax.numpy as jnp
        import numpy as np
        D_IN, D_HID = (128, 512)

        def _ternary(key, shape):
            return jax.random.randint(key, shape, -1, 2).astype(jnp.float32)

        def _tlin(x, w, s):
            return jnp.einsum('bsi,oi->bso', x, w) * s
        h = jax.nn.silu(_tlin(x, w1_w, w1_s)) * _tlin(x, w2_w, w2_s)
        h = jax.nn.gelu(_tlin(h, h1_w, h1_s), approximate=False)
        h = jax.nn.gelu(_tlin(h, h2_w, h2_s), approximate=False)
        return _tlin(h, w3_w, w3_s)

    def _L1_attn_ref(x, Wq, bq, Wk, bk, Wv, bv, Wp, bp, lambda_q1, lambda_k1, lambda_q2, lambda_k2):
        import jax, jax.numpy as jnp
        import numpy as np
        EMBED_DIM = 128
        NUM_HEADS = 16
        EFF_HEADS = NUM_HEADS // 2
        HEAD_DIM = EMBED_DIM // NUM_HEADS
        LAMBDA_INIT = 0.8
        B, N = (2, 256)
        Bb, Nn, C = x.shape
        H, H2, hd = (NUM_HEADS, EFF_HEADS, HEAD_DIM)
        scale = hd ** (-0.5)
        q = (x @ Wq.T + bq).reshape(Bb, Nn, H, hd).transpose(0, 2, 1, 3)
        k = (x @ Wk.T + bk).reshape(Bb, Nn, H, hd).transpose(0, 2, 1, 3)
        v = (x @ Wv.T + bv).reshape(Bb, Nn, H, hd).transpose(0, 2, 1, 3)
        q1, q2 = (q[:, :H2], q[:, H2:])
        k1, k2 = (k[:, :H2], k[:, H2:])
        v1, v2 = (v[:, :H2], v[:, H2:])
        l1 = jnp.exp(jnp.minimum((lambda_q1 * lambda_k1).sum((-1, -2)), 5.0))
        l2 = jnp.exp(jnp.minimum((lambda_q2 * lambda_k2).sum((-1, -2)), 5.0))
        lv = (l1 - l2 + LAMBDA_INIT).mean()
        a1 = jax.nn.softmax(jnp.einsum('bhnd,bhmd->bhnm', q1, k1) * scale, axis=-1)
        x1 = jnp.einsum('bhnm,bhmd->bhnd', a1, v1).transpose(0, 2, 1, 3).reshape(Bb, Nn, C // 2)
        a2 = jax.nn.softmax(jnp.einsum('bhnd,bhmd->bhnm', q2, k2) * scale, axis=-1)
        x2 = jnp.einsum('bhnm,bhmd->bhnd', a2, v2).transpose(0, 2, 1, 3).reshape(Bb, Nn, C // 2)
        out = jnp.concatenate([x1 - lv * x2, x2], axis=-1) @ Wp.T + bp
        return out

    def _L1_ffn_ref(x, switch_w, switch_b, w1, b1, w2, b2):
        import jax, jax.numpy as jnp
        import numpy as np
        B, S, D = (4, 256, 128)
        E, F = (8, 512)
        b, s, d = x.shape
        t = x.reshape(-1, d)
        logits = t @ switch_w + switch_b
        route_prob = jax.nn.softmax(logits, axis=-1)
        route_prob_max = jnp.max(route_prob, axis=-1)
        routes = jnp.argmax(route_prob, axis=-1)
        out = jnp.zeros_like(t)
        n_experts = w1.shape[0]
        for e in range(n_experts):
            h = jax.nn.gelu(t @ w1[e] + b1[e])
            y = h @ w2[e] + b2[e]
            mask = (routes == e)[:, None]
            out = jnp.where(mask, y, out)
        out = out * route_prob_max[:, None]
        return out.reshape(b, s, d)
    x = L0_attn_x
    x = _layernorm(x + _L0_attn_ref(x, L0_attn_in_proj_w, L0_attn_in_proj_b, L0_attn_out_proj_w, L0_attn_out_proj_b, L0_attn_ffn1_w, L0_attn_ffn1_b, L0_attn_ffn2_w, L0_attn_ffn2_b, L0_attn_ln1_w, L0_attn_ln1_b, L0_attn_ln2_w, L0_attn_ln2_b, L0_attn_final_w, L0_attn_final_b), axis=-1)
    x = _layernorm(x + _L0_ffn_ref(x, L0_ffn_w1_w, L0_ffn_w1_s, L0_ffn_w2_w, L0_ffn_w2_s, L0_ffn_h1_w, L0_ffn_h1_s, L0_ffn_h2_w, L0_ffn_h2_s, L0_ffn_w3_w, L0_ffn_w3_s), axis=-1)
    x = _layernorm(x + _L1_attn_ref(x, L1_attn_Wq, L1_attn_bq, L1_attn_Wk, L1_attn_bk, L1_attn_Wv, L1_attn_bv, L1_attn_Wp, L1_attn_bp, L1_attn_lambda_q1, L1_attn_lambda_k1, L1_attn_lambda_q2, L1_attn_lambda_k2), axis=-1)
    x = _layernorm(x + _L1_ffn_ref(x, L1_ffn_switch_w, L1_ffn_switch_b, L1_ffn_w1, L1_ffn_b1, L1_ffn_w2, L1_ffn_b2), axis=-1)
    return x

_drawn_inputs = setup_inputs


def setup_inputs(seed=0):
    import zlib

    import numpy as np

    out = dict(_drawn_inputs(seed))
    spreads = {'L0_attn_in_proj_b': (0.0, 0.1),
     'L0_attn_out_proj_b': (0.0, 0.1),
     'L0_attn_ffn1_b': (0.0, 0.1),
     'L0_attn_ffn2_b': (0.0, 0.1),
     'L0_attn_ln1_w': (1.0, 0.6),
     'L0_attn_ln1_b': (0.0, 0.585),
     'L0_attn_ln2_w': (1.0, 0.6),
     'L0_attn_ln2_b': (0.0, 0.538),
     'L0_attn_final_w': (1.0, 0.2),
     'L0_attn_final_b': (0.0, 0.1),
     'L1_attn_bq': (0.0, 0.8),
     'L1_attn_bk': (0.0, 2.0),
     'L1_attn_bv': (0.0, 0.1),
     'L1_attn_bp': (0.0, 0.1),
     'L1_ffn_switch_b': (0.0, 0.1),
     'L1_ffn_b1': (0.0, 0.306),
     'L1_ffn_b2': (0.0, 0.1)}
    factors = {'L0_ffn_w1_w': 6.364,
     'L0_ffn_w1_s': 6.939,
     'L0_ffn_w2_w': 5.762,
     'L0_ffn_w2_s': 8.0,
     'L0_ffn_h1_w': 4.744,
     'L0_ffn_h1_s': 8.0,
     'L0_ffn_h2_w': 5.703,
     'L0_ffn_h2_s': 7.268,
     'L0_ffn_w3_w': 5.477,
     'L0_ffn_w3_s': 6.958,
     'L1_attn_Wq': 8.0,
     'L1_attn_Wk': 8.0,
     'L1_attn_Wv': 3.035,
     'L1_attn_lambda_q1': 64.0,
     'L1_attn_lambda_k1': 39.696,
     'L1_attn_lambda_q2': 43.439,
     'L1_attn_lambda_k2': 46.63}
    for name, (base, spread) in spreads.items():
        noise = np.random.default_rng([zlib.crc32(name.encode()), seed]).standard_normal(out[name].shape)
        drawn = base * np.exp(spread * noise) if base else spread * noise
        out[name] = jnp.asarray(drawn.astype(out[name].dtype))
    for name, factor in factors.items():
        out[name] = (out[name] * factor).astype(out[name].dtype)
    return out
```

```python
import concourse.bass as bass
from concourse import mybir
from contextlib import ExitStack
import numpy as np

F32 = mybir.dt.float32
BF16 = mybir.dt.bfloat16
ALU = mybir.AluOpType
ACT = mybir.ActivationFunctionType
AX = mybir.AxisListType

P = 128
B, T, D = 4, 1024, 128
LAYERS = 4
HEADS, HD = 16, 8
PAIRS = HEADS // 2
FF = 512
FT = FF // P
EXPERTS = 8
QT = T // P
HALF = T // 2
EPS = 1e-5
SCALE = HD ** -0.5
LAMBDA_INIT = 0.8

HROWS = 64
Q_PARTS = (0, 0, 0, 1, 2, 1)
K_PARTS = (1, 2, 0, 0, 0, 1)
PART_ROWS = len(Q_PARTS) * HD
ALIBI_ROW = PART_ROWS
MAX_ROW = ALIBI_ROW + 6
EXTRA_ROWS = HROWS - PART_ROWS
BLOCKS = HROWS // HD
EARLY = 4 * HD
MASKED = -1e30
LOWEST = -3e38

LN1_W, LN1_B, LN2_W, LN2_B, BQ, BK, B1 = 0, 1, 2, 3, 4, 5, 6
N_COLS = B1 + FT
BV, BO, B2 = 0, 1, 2
S_W1, S_W2, S_H1, S_H2, T_BQ, T_BK = 0, 4, 8, 12, 16, 17
N_TCOLS = 18
FIN_W, FIN_B, S_W3, T_BV, T_BP = range(5)


def build(nc, x_in, layer_wi, layer_wo, layer_f1, layer_f2, layer_cols, layer_rows,
          tern_w1, tern_w2, tern_h1, tern_h2, tern_w3, tail_cols, tail_rows,
          diff_w, diff_wp, lambdas, switch_w, switch_b, moe_w1, moe_b1, moe_w2, moe_b2,
          ident_in, identb_in, causal_in, later_in, q_extra, k_extra, out):
    ctx = ExitStack()
    with ctx:
        def sb(name, shape, dt=F32):
            return ctx.enter_context(nc.sbuf_tensor(name, shape, dt))

        ident = sb("ident", [P, P])
        identb = sb("identb", [P, P], BF16)
        causal = sb("causal", [P, 4 * P])
        later = sb("later", [P, P], BF16)
        zeros = sb("zeros", [P, P])
        neg_half = sb("neg_half", [P, QT])
        minus_one = sb("minus_one", [P, 4, 2])
        rank = sb("rank", [P, EXPERTS])
        wi = sb("wi", [P, 3 * D])
        wo = sb("wo", [P, D])
        f1 = sb("f1", [P, FF])
        f2 = sb("f2", [P, FT, D])
        cols = sb("cols", [P, N_COLS])
        rows = sb("rows", [P, 3, D])
        next_cols = sb("next_cols", [P, N_COLS])
        next_rows = sb("next_rows", [P, 3, D])
        tw1 = sb("tw1", [P, FF])
        tw2 = sb("tw2", [P, FF])
        th1 = sb("th1", [P, FT, FF])
        th2 = sb("th2", [P, FT, FF])
        tw3 = sb("tw3", [P, FT, D])
        tcols = sb("tcols", [P, N_TCOLS])
        trows = sb("trows", [P, 5, D])
        dwi = sb("dwi", [P, 3 * D])
        dwo = sb("dwo", [P, D])
        lam = sb("lam", [P, 4, HEADS // 2, HD])
        lam_work = sb("lam_work", [P, 2, HEADS // 2, HD])
        lam_sum = sb("lam_sum", [P, 2, HEADS // 2])
        lam_exp = sb("lam_exp", [P, 2, HEADS // 2])
        lam_mean = sb("lam_mean", [P, 4])
        sw = sb("sw", [P, EXPERTS])
        swb = sb("swb", [P, EXPERTS])
        ew1 = sb("ew1", [P, 2, FF])
        ew2 = sb("ew2", [P, 2, FT, D])
        eb1 = sb("eb1", [P, EXPERTS, FT])
        eb2 = sb("eb2", [P, EXPERTS, D])
        xs = [sb(f"x{w}", [P, QT, D]) for w in range(2)]
        xb = sb("xb", [P, QT, D])
        xhat = sb("xhat", [P, QT, D])
        xnT = sb("xnT", [P, T])
        stats = sb("stats", [P, QT, 6])
        mv = sb("mv", [P, QT, 2])
        var_eps = sb("var_eps", [P, QT])
        rstd = sb("rstd", [P, QT])
        v_augs = [sb(f"v_aug{w}", [P, QT, HEADS, HD + 1]) for w in range(2)]
        attns = [sb(f"attn{w}", [P, QT, D]) for w in range(2)]
        hidden = sb("hidden", [P, 8 * T])
        hidA = hidden[:, 0:FT * T].rearrange("p (f t) -> p f t", f=FT)
        hidB = hidden[:, FT * T:2 * FT * T].rearrange("p (f t) -> p f t", f=FT)
        q32, k32 = hidden[:, 0:T], hidden[:, T:2 * T]
        q_part = hidden[:, FT * T:FT * T + 3 * T // 2].bitcast(BF16).rearrange("p (n t) -> p n t", n=3)
        k_part = hidden[:, FT * T + 3 * T // 2:FT * T + 3 * T].bitcast(BF16).rearrange("p (n t) -> p n t", n=3)
        probs = sb("probs", [P, 4, 2, HALF])
        KM = sb("k_pass_one", [P, 2, T], BF16)
        KS = sb("k_pass_two", [P, 2, T], BF16)
        QM = sb("q_pass_one", [P, 2, 2, T], BF16)
        QS = sb("q_pass_two", [P, 2, 2, T], BF16)
        v_pair = sb("v_pair", [P, 2, QT, 2, HD + 1])
        o_sb = sb("o_sb", [P, 2, HALF])
        parts = sb("parts", [P, 2, 4, 2, 2])
        neg_max = sb("neg_max", [P, 2, 4, 2])
        max_bf = sb("max_bf", [P, 2, 2, 2, 4], BF16)
        maxT = sb("maxT", [16, 2, P], BF16)
        masked_out = sb("masked_out", [P, 4, 4 * P])
        o_turned = sb("o_turned", [P, 2, 4, 2, 2, HD + 1])
        o_sum = sb("o_sum", [P, 2, 4, 2, HD + 1])
        o_rec = sb("o_rec", [P, 2, 4, 2])
        logit = sb("logit", [P, QT, EXPERTS])
        lmax = sb("lmax", [P, QT])
        lexp = sb("lexp", [P, QT, EXPERTS])
        lsum = sb("lsum", [P, QT])
        prob = sb("prob", [P, QT, EXPERTS])
        gate = sb("gate", [P, QT, EXPERTS])

        psum = ctx.enter_context(nc.psum_tensor("psum", [P, 8 * 512], F32))

        def bank(i, n=1):
            return psum[:, i * 512:(i + n) * 512]

        q_rows = nc.dram_tensor("q_rows", (4, BLOCKS, D, T), BF16, kind="Internal").ap()
        k_rows = nc.dram_tensor("k_rows", (4, BLOCKS, D, T), BF16, kind="Internal").ap()

        def signals(stage, names):
            sems = {n: ctx.enter_context(nc.semaphore(f"{stage}_{n}")) for n in names.split()}
            return sems

        def clear(eng, stages):
            for stage in stages:
                for sem in stage.values():
                    eng.sem_clear(sem)

        waited = ctx.enter_context(nc.semaphore("waited"))
        LN = " stats moments var rstd xhat"
        S0 = signals("setup", "loaded written memset lambda_step lambda_exp")
        SL = signals("load", "x")
        ATT = ("load ring_full ring_free st_full exp_done pv_done v_staged o_evac o_step normed"
               " max_ready max_step max_found m_loaded0 m_loaded1 s_loaded0 s_loaded1 max_rows0 max_rows1")
        SPROJ = signals("project", "loaded turned xnT qk v q32 k32 part1 rest part2 part3 v_ready written written_rest" + LN)
        SATT = [signals(f"attention{w}", ATT) for w in range(2)]
        SIDE = [signals(f"side{w}", "full free loaded bias bias2 gelu part1 rest part2 part3 written" + LN)
                for w in range(2)]
        SF = signals("differential", "mixed attn_turned attnT bias proj resid normed scaled x0 sum" + LN)
        ST = signals("tern", "turned xnT gate up silu hidden h1 g1 h2 g2 w3 scaled sum" + LN)
        SM = signals("moe", "turned xnT loaded0 loaded1 logits step gate hidden gelu y tmp acc stored lexp" + LN)
        SR, SR2 = SF, SM

        def wait_alone(eng, sem, value):
            eng.wait_ge(sem, value)
            if not isinstance(value, int):
                eng.sem_inc(waited, 1)

        def layer_norm_vector(v, s, src, dst):
            for t in range(QT):
                nc.vector.bn_stats(stats[:, t, :], src[:, t, :]).then_inc(s["stats"], 1)
            v.wait_ge(s["stats"], QT)
            for t in range(QT):
                nc.vector.bn_aggr(mv[:, t, :], stats[:, t, :]).then_inc(s["moments"], 1)
            v.wait_ge(s["moments"], QT)
            nc.vector.tensor_scalar(var_eps[:, :], mv[:, :, 1], EPS, None, ALU.add).then_inc(s["var"], 1)
            v.wait_ge(s["rstd"], 1)
            for t in range(QT):
                nc.vector.tensor_scalar(dst[:, t, :], src[:, t, :], mv[:, t, 0:1], rstd[:, t:t + 1],
                                        ALU.subtract, ALU.mult).then_inc(s["xhat"], 1)

        def layer_norm_pool(g, s):
            g.wait_ge(s["var"], 1)
            nc.gpsimd.tensor_tensor(rstd[:, :], var_eps[:, :], neg_half[:, :], ALU.pow).then_inc(s["rstd"], 1)

        def turn_tensor(pe, ready, signal, src, b0):
            for t in range(QT):
                if ready is not None:
                    pe.wait_ge(ready, t + 1)
                nc.tensor.transpose(bank(b0 + t // 4)[:, (t % 4) * P:(t % 4 + 1) * P], src[:, t, :],
                                    ident[:, :]).then_inc(signal, 1)

        with nc.Block() as block:
            LOADS = [(ident, ident_in), (identb, identb_in), (causal, causal_in), (later, later_in),
                     (tw1, tern_w1), (tw2, tern_w2), (th1, tern_h1), (th2, tern_h2), (tw3, tern_w3),
                     (tcols, tail_cols), (sw, switch_w), (eb1, moe_b1), (dwi, diff_w), (dwo, diff_wp)]
            SPREAD = [(trows, tail_rows), (lam, lambdas), (swb, switch_b), (eb2, moe_b2)]

            @block.sync
            def _(sp):
                for dst, src in LOADS:
                    sp.dma_start(dst[:], src).then_inc(S0["loaded"], 16)
                for dst, src in SPREAD:
                    sp.dma_start(dst[:], src).then_inc(S0["loaded"], 16)
                for i in range(4):
                    sp.dma_start(q_rows[i, len(Q_PARTS):], q_extra[i // 2]).then_inc(S0["written"], 16)
                    sp.dma_start(k_rows[i, len(Q_PARTS):], k_extra).then_inc(S0["written"], 16)
                sp.wait_ge(S0["loaded"], 16 * (len(LOADS) + len(SPREAD)))
                sp.wait_ge(S0["written"], 16 * 8)

            @block.gpsimd
            def _(g):
                nc.gpsimd.memset(QM[:], 0.0).then_inc(S0["memset"], 1)
                nc.gpsimd.memset(QS[:], 0.0).then_inc(S0["memset"], 1)
                nc.gpsimd.memset(zeros[:], 0.0).then_inc(S0["memset"], 1)
                nc.gpsimd.memset(minus_one[:], -1.0).then_inc(S0["memset"], 1)
                nc.gpsimd.memset(neg_half[:], -0.5).then_inc(S0["memset"], 1)
                for e in range(EXPERTS):
                    nc.gpsimd.memset(rank[:, e:e + 1], float(EXPERTS - e)).then_inc(S0["memset"], 1)
                for v_aug in v_augs:
                    nc.gpsimd.memset(v_aug[:, :, :, HD:HD + 1], 1.0).then_inc(S0["memset"], 1)

            @block.vector
            def _(v):
                v.wait_ge(S0["loaded"], 16 * (len(LOADS) + len(SPREAD)))
                for i in range(2):
                    nc.vector.tensor_tensor(lam_work[:, i], lam[:, 2 * i], lam[:, 2 * i + 1],
                                            ALU.mult).then_inc(S0["lambda_step"], 1)
                v.wait_ge(S0["lambda_step"], 2)
                nc.vector.tensor_reduce(lam_sum[:, :, :], lam_work[:, :, :, :], op=ALU.add, axis=AX.X).then_inc(S0["lambda_step"], 1)
                v.wait_ge(S0["lambda_step"], 3)
                nc.vector.tensor_scalar(lam_sum[:, :, :], lam_sum[:, :, :], 5.0, None, ALU.min).then_inc(S0["lambda_step"], 1)
                v.wait_ge(S0["lambda_exp"], 1)
                nc.vector.tensor_reduce(lam_mean[:, 0:2], lam_exp[:, :, :], op=ALU.add, axis=AX.X).then_inc(S0["lambda_step"], 1)
                v.wait_ge(S0["lambda_step"], 5)
                nc.vector.tensor_tensor(lam_mean[:, 2:3], lam_mean[:, 1:2], lam_mean[:, 0:1],
                                        ALU.subtract).then_inc(S0["lambda_step"], 1)
                v.wait_ge(S0["lambda_step"], 6)
                nc.vector.tensor_scalar(lam_mean[:, 3:4], lam_mean[:, 2:3], 2.0 / HEADS, -LAMBDA_INIT,
                                        ALU.mult, ALU.add).then_inc(S0["lambda_step"], 1)

            @block.scalar
            def _(a):
                a.wait_ge(S0["lambda_step"], 4)
                nc.scalar.activation(lam_exp[:, :, :], lam_sum[:, :, :], ACT.Exp).then_inc(S0["lambda_exp"], 1)

        def write_parts(sp, kind, w, part, first, last, signal):
            for src, dst, order in ((q_part, q_rows, Q_PARTS), (k_part, k_rows, K_PARTS)):
                blocks = [i for i in range(len(order)) if order[i] == part]
                step = blocks[1] - blocks[0] if len(blocks) > 1 else 1
                sp.dma_start(dst[2 * kind + w, blocks[0]:blocks[-1] + 1:step, first:last, :]
                             .rearrange("b r t -> r b t"),
                             src[first:last, part, :].unsqueeze(1)
                             .broadcast_to([last - first, len(blocks), T])).then_inc(signal, 16)

        def project_stage(kind, w, clears):
            s = SPROJ
            x, v_aug = xs[w], v_augs[w]
            causal_kind = kind == 0
            bq = next_cols[:, BQ:BQ + 1] if causal_kind else tcols[:, T_BQ:T_BQ + 1]
            bk = next_cols[:, BK:BK + 1] if causal_kind else tcols[:, T_BK:T_BK + 1]
            bv = next_rows[:, BV, :] if causal_kind else trows[:, T_BV, :]
            w_qkv = wi if causal_kind else dwi
            with nc.Block() as block:
                @block.sync
                def _(sp):
                    clear(sp, clears)
                    if causal_kind:
                        for dst, src in ((next_cols, layer_cols), (wi, layer_wi), (next_rows, layer_rows)):
                            sp.dma_start(dst[:], src[0]).then_inc(s["loaded"], 16)
                    for part in range(3):
                        sp.wait_ge(s[("part1", "part2", "part3")[part]], 4)
                        write_parts(sp, kind, w, part, 0, EARLY, s["written"])

                @block.vector
                def _(v):
                    if causal_kind:
                        layer_norm_vector(v, s, x, xhat)
                    if causal_kind:
                        v.wait_ge(s["loaded"], 16 * 3)
                    for h in range(2):
                        v.wait_ge(s["qk"], 2 * h + 1)
                        nc.vector.tensor_scalar(q32[:, h * HALF:(h + 1) * HALF], bank(2 + h), bq, SCALE,
                                                ALU.add, ALU.mult).then_inc(s["q32"], 1)
                    n = 0
                    for h in range(2):
                        hs = slice(h * HALF, (h + 1) * HALF)
                        for i, (full, part) in enumerate(((q32, q_part), (k32, k_part))):
                            v.wait_ge(s["part1"], 2 * h + i + 1)
                            nc.vector.tensor_tensor(full[:, hs], full[:, hs], part[:, 0, hs],
                                                    ALU.subtract).then_inc(s["rest"], 1)
                    for h in range(2):
                        hs = slice(h * HALF, (h + 1) * HALF)
                        for i, (full, part) in enumerate(((q32, q_part), (k32, k_part))):
                            v.wait_ge(s["part2"], 2 * h + i + 1)
                            nc.vector.tensor_tensor(part[:, 2, hs], full[:, hs], part[:, 1, hs],
                                                    ALU.subtract).then_inc(s["part3"], 1)
                    for t in range(QT):
                        v.wait_ge(s["v"], 4 * (t // 4 + 1))
                        nc.vector.tensor_tensor(v_aug[:, t, :, 0:HD],
                                                bank(6 + t // 4)[:, (t % 4) * P:(t % 4 + 1) * P]
                                                .rearrange("p (h d) -> p h d", h=HEADS),
                                                bv.rearrange("p (h d) -> p h d", h=HEADS),
                                                ALU.add).then_inc(s["v_ready"], 1)

                @block.gpsimd
                def _(g):
                    if causal_kind:
                        layer_norm_pool(g, s)

                @block.tensor
                def _(pe):
                    if causal_kind:
                        turn_tensor(pe, s["xhat"], s["turned"], xhat, 0)
                    else:
                        turn_tensor(pe, None, s["turned"], x, 0)
                    if causal_kind:
                        pe.wait_ge(s["loaded"], 16 * 3)
                    for h in range(2):
                        pe.wait_ge(s["xnT"], h + 1)
                        for o in range(2):
                            nc.tensor.matmul(bank(2 + 2 * o + h), w_qkv[:, o * D:(o + 1) * D],
                                             xnT[:, h * HALF:(h + 1) * HALF],
                                             start=True, stop=True).then_inc(s["qk"], 1)
                    for t in range(QT):
                        nc.tensor.matmul(bank(6 + t // 4)[:, (t % 4) * P:(t % 4 + 1) * P],
                                         xnT[:, t * P:(t + 1) * P], w_qkv[:, 2 * D:3 * D],
                                         start=True, stop=True).then_inc(s["v"], 1)

                @block.scalar
                def _(a):
                    if causal_kind:
                        a.wait_ge(s["loaded"], 16 * 3)
                    for h in range(2):
                        a.wait_ge(s["turned"], 4 * (h + 1))
                        hs = slice(h * HALF, (h + 1) * HALF)
                        if causal_kind:
                            nc.scalar.activation(xnT[:, hs], bank(h), ACT.Identity, bias=next_cols[:, LN1_B:LN1_B + 1],
                                                 scale=next_cols[:, LN1_W:LN1_W + 1]).then_inc(s["xnT"], 1)
                        else:
                            nc.scalar.activation(xnT[:, hs], bank(h), ACT.Identity).then_inc(s["xnT"], 1)
                    for h in range(2):
                        hs = slice(h * HALF, (h + 1) * HALF)
                        a.wait_ge(s["qk"], 2 * h + 2)
                        nc.scalar.activation(k32[:, hs], bank(4 + h), ACT.Identity, bias=bk).then_inc(s["k32"], 1)
                        a.wait_ge(s["q32"], h + 1)
                        nc.scalar.activation(q_part[:, 0, hs], q32[:, hs], ACT.Identity).then_inc(s["part1"], 1)
                        a.wait_ge(s["k32"], h + 1)
                        nc.scalar.activation(k_part[:, 0, hs], k32[:, hs], ACT.Identity).then_inc(s["part1"], 1)
                    for h in range(2):
                        hs = slice(h * HALF, (h + 1) * HALF)
                        for i, (full, part) in enumerate(((q32, q_part), (k32, k_part))):
                            a.wait_ge(s["rest"], 2 * h + i + 1)
                            nc.scalar.activation(part[:, 1, hs], full[:, hs], ACT.Identity).then_inc(s["part2"], 1)

        def side_entries(entries, item, tick, pace):
            table = {}
            for name, items, ticks in entries:
                table[name] = (tick, item)
                item += items
                tick += ticks * pace if items else ticks
            return table, item, tick

        NORM_TICKS = 10
        SIDE_BANK = 7
        FFN_STEPS = ([(("turn", h), 1, 1) for h in range(2)] + [(("proj", h), 1, 1) for h in range(2)]
                     + [("norm", 0, NORM_TICKS)] + [(("turn_norm", h), 1, 1) for h in range(2)]
                     + [(("hidden", n), 1, 1) for n in range(2 * FT)]
                     + [("gap", 0, 1), (("ffn2", 0), 1, 2), ("gap2", 0, 3), (("ffn2", 1), 1, 2)])
        PROJECT_STEPS = ([("norm", 0, NORM_TICKS)] + [(("turn", h), 1, 1) for h in range(2)]
                         + [((o, h), 1, 1) for h in range(2) for o in ("q", "k")]
                         + [(("v", h), 1, 1) for h in range(2)] + [("split", 0, 4), ("end", 0, 3)])

        def side_norm(v, s, src, dst, norms, tick):
            for h in range(2):
                yield tick + h
                for t in range(4 * h, 4 * h + 4):
                    nc.vector.bn_stats(stats[:, t, :], src[:, t, :]).then_inc(s["stats"], 1)
            v.wait_ge(s["stats"], QT * (norms + 1))
            for t in range(QT):
                nc.vector.bn_aggr(mv[:, t, :], stats[:, t, :]).then_inc(s["moments"], 1)
            v.wait_ge(s["moments"], QT * (norms + 1))
            nc.vector.tensor_scalar(var_eps[:, :], mv[:, :, 1], EPS, None, ALU.add).then_inc(s["var"], 1)
            for h in range(2):
                yield tick + NORM_TICKS - 2 + h
                v.wait_ge(s["rstd"], norms + 1)
                for t in range(4 * h, 4 * h + 4):
                    nc.vector.tensor_scalar(dst[:, t, :], src[:, t, :], mv[:, t, 0:1], rstd[:, t:t + 1],
                                            ALU.subtract, ALU.mult).then_inc(s["xhat"], 1)

        def side_norm_pool(g, s, norms, tick):
            yield tick + 2
            g.wait_ge(s["var"], norms + 1)
            nc.gpsimd.tensor_tensor(rstd[:, :], var_eps[:, :], neg_half[:, :], ALU.pow).then_inc(s["rstd"], 1)

        class Side:

            def __init__(self, w, layer, ffn, project, load, start, pace, parts_free=None):
                self.w, self.layer, self.ffn, self.project, self.load = w, layer, ffn, project, load
                self.parts_free = parts_free
                item, tick = 0, start
                if ffn:
                    self.F, item, tick = side_entries(FFN_STEPS, item, tick, pace)
                if project:
                    self.J, item, tick = side_entries(PROJECT_STEPS, item, tick, pace)
                self.end = tick

            def loads(self):
                ffn_loads = [(cols, layer_cols, 0), (rows, layer_rows, 0), (wo, layer_wo, 0), (f1, layer_f1, 0),
                             (f2, layer_f2, 0)] if self.ffn else []
                return ffn_loads + ([(wi, layer_wi, 1), (next_cols, layer_cols, 1), (next_rows, layer_rows, 1)]
                                    if self.project else [])

            def sync(self, sp):
                s = SIDE[self.w]
                if self.load:
                    yield 0
                    for dst, src, ahead in self.loads():
                        sp.dma_start(dst[:], src[self.layer + ahead]).then_inc(s["loaded"], 16)
                if self.project:
                    for part in range(3):
                        yield (self.J["v", 1][0], self.J["end"][0], self.J["end"][0] + 3)[part]
                        sp.wait_ge(s[("part1", "part2", "part3")[part]], 4)
                        write_parts(sp, 0, self.w, part, 0, D, s["written"])
                    sp.wait_ge(s["written"], 16 * 6)

            def tensor(self, pe):
                s, w = SIDE[self.w], self.w
                dst = bank(SIDE_BANK)

                def due(step):
                    if step[1]:
                        pe.wait_ge(s["free"], step[1])

                def turn(src, h):
                    for t in range(4 * h, 4 * h + 4):
                        mm = nc.tensor.transpose(dst[:, token_rows(t)], src[:, t, :], ident[:, :])
                    mm.then_inc(s["full"], 1)

                if self.load:
                    pe.wait_ge(s["loaded"], 16 * len(self.loads()))
                if self.ffn:
                    for h in range(2):
                        yield self.F["turn", h][0]
                        due(self.F["turn", h])
                        turn(attns[w], h)
                    for h in range(2):
                        yield self.F["proj", h][0]
                        due(self.F["proj", h])
                        for t in range(4 * h, 4 * h + 4):
                            mm = nc.tensor.matmul(dst[:, token_rows(t)], xnT[:, t * P:(t + 1) * P], wo[:, :],
                                                  start=True, stop=True)
                        mm.then_inc(s["full"], 1)
                    for h in range(2):
                        yield self.F["turn_norm", h][0]
                        due(self.F["turn_norm", h])
                        pe.wait_ge(s["xhat"], 4 * (h + 1))
                        turn(xhat, h)
                    for n in range(2 * FT):
                        h, f = n // FT, n % FT
                        yield self.F["hidden", n][0]
                        due(self.F["hidden", n])
                        nc.tensor.matmul(dst, f1[:, f * P:(f + 1) * P], xnT[:, h * HALF:(h + 1) * HALF],
                                         start=True, stop=True).then_inc(s["full"], 1)
                    for h in range(2):
                        yield self.F["ffn2", h][0]
                        due(self.F["ffn2", h])
                        pe.wait_ge(s["gelu"], h + 1)
                        for t in range(4 * h, 4 * h + 4):
                            if t % 2 == 0 and t % 4:
                                yield self.F["ffn2", h][0] + 1
                            for f in range(FT):
                                mm = nc.tensor.matmul(dst[:, token_rows(t)], hidA[:, f, t * P:(t + 1) * P],
                                                      f2[:, f, :], start=f == 0, stop=f == FT - 1)
                        mm.then_inc(s["full"], 1)
                if self.project:
                    for h in range(2):
                        yield self.J["turn", h][0]
                        due(self.J["turn", h])
                        pe.wait_ge(s["xhat"], QT * self.ffn + 4 * (h + 1))
                        turn(xhat, h)
                    for h in range(2):
                        for o, name in enumerate("qk"):
                            yield self.J[name, h][0]
                            due(self.J[name, h])
                            nc.tensor.matmul(dst, wi[:, o * D:(o + 1) * D], xnT[:, h * HALF:(h + 1) * HALF],
                                             start=True, stop=True).then_inc(s["full"], 1)
                    for h in range(2):
                        yield self.J["v", h][0]
                        due(self.J["v", h])
                        for t in range(4 * h, 4 * h + 4):
                            mm = nc.tensor.matmul(dst[:, token_rows(t)], xnT[:, t * P:(t + 1) * P],
                                                  wi[:, 2 * D:3 * D], start=True, stop=True)
                        mm.then_inc(s["full"], 1)

            def scalar(self, a):
                s = SIDE[self.w]
                src = bank(SIDE_BANK)

                def copy(dst, step, scale=1.0, bias=0.0):
                    a.wait_ge(s["full"], step[1] + 1)
                    nc.scalar.activation(dst, src, ACT.Identity, bias=bias, scale=scale).then_inc(s["free"], 1)

                if self.ffn:
                    for h in range(2):
                        yield self.F["turn", h][0] + 0.5
                        copy(xnT[:, h * HALF:(h + 1) * HALF], self.F["turn", h])
                    for h in range(2):
                        yield self.F["turn_norm", h][0] + 0.5
                        copy(xnT[:, h * HALF:(h + 1) * HALF], self.F["turn_norm", h],
                             cols[:, LN2_W:LN2_W + 1], cols[:, LN2_B:LN2_B + 1])
                    for h in range(2):
                        last = self.F["hidden", FT * (h + 1) - 1]
                        yield last[0] + 2
                        a.wait_ge(s["free"], last[1] + 1)
                        hs = slice(h * HALF, (h + 1) * HALF)
                        nc.scalar.activation(hidA[:, :, hs], hidA[:, :, hs], ACT.Gelu).then_inc(s["gelu"], 1)
                if self.project:
                    for h in range(2):
                        yield self.J["turn", h][0] + 0.5
                        copy(xnT[:, h * HALF:(h + 1) * HALF], self.J["turn", h],
                             next_cols[:, LN1_W:LN1_W + 1], next_cols[:, LN1_B:LN1_B + 1])
                    for h in range(2):
                        hs = slice(h * HALF, (h + 1) * HALF)
                        yield self.J["k", h][0] + 0.5
                        copy(k32[:, hs], self.J["k", h], bias=next_cols[:, BK:BK + 1])
                        if h == 0 and self.parts_free:
                            a.wait_ge(*self.parts_free)
                        a.wait_ge(s["free"], self.J["k", h][1] + 1)
                        for full_, part in ((q32, q_part), (k32, k_part)):
                            nc.scalar.activation(part[:, 0, hs], full_[:, hs], ACT.Identity).then_inc(s["part1"], 1)
                            yield self.J["k", h][0] + 1
                    for h in range(2):
                        hs = slice(h * HALF, (h + 1) * HALF)
                        for i, (full_, part) in enumerate(((q32, q_part), (k32, k_part))):
                            yield self.J["v", h][0] + 2 + i
                            a.wait_ge(s["rest"], 2 * h + i + 1)
                            nc.scalar.activation(part[:, 1, hs], full_[:, hs], ACT.Identity).then_inc(s["part2"], 1)

            def gpsimd(self, g):
                s, x = SIDE[self.w], xs[self.w]
                if self.ffn:
                    yield 0
                    if self.load:
                        g.wait_ge(s["loaded"], 16 * len(self.loads()))
                    nc.gpsimd.tensor_tensor(xb[:, :, :], x[:, :, :], over_tiles(rows[:, BO, :], QT), ALU.add)\
                        .then_inc(s["bias"], 1)
                    yield from side_norm_pool(g, s, 0, self.F["norm"][0])
                    g.wait_ge(s["free"], self.F["proj", 1][1] + 1)
                    nc.gpsimd.tensor_tensor(xb[:, :, :], x[:, :, :], over_tiles(rows[:, B2, :], QT), ALU.add)\
                        .then_inc(s["bias2"], 1)
                if self.project:
                    yield from side_norm_pool(g, s, int(self.ffn), self.J["norm"][0])

            def vector(self, v):
                s, x, v_aug = SIDE[self.w], xs[self.w], v_augs[self.w]
                src = bank(SIDE_BANK)

                def add_up(step, h, ready):
                    v.wait_ge(s[ready], 1)
                    v.wait_ge(s["full"], step[1] + 1)
                    nc.vector.tensor_tensor(x[:, 4 * h:4 * h + 4, :], xb[:, 4 * h:4 * h + 4, :],
                                            tokens(src), ALU.add).then_inc(s["free"], 1)

                if self.ffn:
                    for h in range(2):
                        yield self.F["proj", h][0] + 0.5
                        add_up(self.F["proj", h], h, "bias")
                    v.wait_ge(s["free"], self.F["proj", 1][1] + 1)
                    yield from side_norm(v, s, x, xhat, 0, self.F["norm"][0])
                    for n in range(2 * FT):
                        h, f = n // FT, n % FT
                        yield self.F["hidden", n][0] + 0.5
                        v.wait_ge(s["full"], self.F["hidden", n][1] + 1)
                        nc.vector.tensor_scalar(hidA[:, f, h * HALF:(h + 1) * HALF], src,
                                                cols[:, B1 + f:B1 + f + 1], None, ALU.add).then_inc(s["free"], 1)
                    for h in range(2):
                        yield self.F["ffn2", h][0] + 1.5
                        add_up(self.F["ffn2", h], h, "bias2")
                    v.wait_ge(s["free"], self.F["ffn2", 1][1] + 1)
                if self.project:
                    yield from side_norm(v, s, x, xhat, int(self.ffn), self.J["norm"][0])
                    for h in range(2):
                        yield self.J["q", h][0] + 0.5
                        v.wait_ge(s["full"], self.J["q", h][1] + 1)
                        nc.vector.tensor_scalar(q32[:, h * HALF:(h + 1) * HALF], src, next_cols[:, BQ:BQ + 1], SCALE,
                                                ALU.add, ALU.mult).then_inc(s["free"], 1)
                    for h in range(2):
                        hs = slice(h * HALF, (h + 1) * HALF)
                        yield self.J["v", h][0] + 0.5
                        v.wait_ge(s["full"], self.J["v", h][1] + 1)
                        nc.vector.tensor_tensor(
                            v_aug[:, 4 * h:4 * h + 4, :, 0:HD],
                            tokens(src).rearrange("p t (h d) -> p t h d", h=HEADS),
                            next_rows[:, BV, :].rearrange("p (h d) -> p h d", h=HEADS).unsqueeze(1)
                            .broadcast_to([P, 4, HEADS, HD]), ALU.add).then_inc(s["free"], 1)
                        for i, (full_, part) in enumerate(((q32, q_part), (k32, k_part))):
                            v.wait_ge(s["part1"], 2 * h + i + 1)
                            nc.vector.tensor_tensor(full_[:, hs], full_[:, hs], part[:, 0, hs],
                                                    ALU.subtract).then_inc(s["rest"], 1)
                    for h in range(2):
                        hs = slice(h * HALF, (h + 1) * HALF)
                        for i, (full_, part) in enumerate(((q32, q_part), (k32, k_part))):
                            yield self.J["end"][0] + 0.5 + h
                            v.wait_ge(s["part2"], 2 * h + i + 1)
                            nc.vector.tensor_tensor(part[:, 2, hs], full_[:, hs], part[:, 1, hs],
                                                    ALU.subtract).then_inc(s["part3"], 1)

        def beside(generator):
            pending = [0]

            def run(tick):
                while pending[0] is not None and pending[0] <= tick:
                    pending[0] = next(generator, None)
            return run

        def attention_stage(kind, w, clears, fresh=False, side=None):
            s, v_aug, attn = SATT[w], v_augs[w], attns[w]
            full = kind == 1
            HALF_TILES = (QT, QT if full else QT // 2)
            NC = sum(HALF_TILES)
            NS = 2 * NC
            NG = NC // 2
            DIAG = [] if full else [4, 5, 6, 7, 8, 9, 10, 11]
            MT1, MT0, OT0, OT1 = 9, 3, 4, 11
            m_loaded, s_loaded, max_sent = ((s["m_loaded0"], s["m_loaded1"]), (s["s_loaded0"], s["s_loaded1"]),
                                            (s["max_rows0"], s["max_rows1"]))

            def loads(u, par):
                return 32 * u + 64 - 32 * par

            def chunk(c):
                half, j = (1, c) if c < QT else (0, c - QT)
                return half, j, 0 if full else max(0, (j - 4 * half) * P)

            def score(i):
                if i < 16:
                    half, r, h, kb = 1, i // 4, (i // 2) % 2, i % 2
                elif full:
                    half, r, h, kb = 0, (i - 16) // 4, (i // 2) % 2, i % 2
                else:
                    half, r, h, kb = 0, (i - 16) // 2, i % 2, 0
                return half, r, h, kb, (r + 1) * P if (not full and kb == half) else 4 * P

            def flags(where):
                cur = where in ("first", "inner", "last")
                nxt = where in ("before", "first", "inner")
                prev = where in ("inner", "last", "after")
                return cur, nxt, prev

            RING = 3
            RING_BANKS = (0, 1, 2)
            ST_RING = 3
            OT_TILES = 4 if full else 2

            def ring_items(where):
                cur, nxt, prev = flags(where)
                place, slots_ = 0, []
                for c in range(NC):
                    items = []
                    if cur and c == MT0:
                        items.append(("max0", 0))
                    if nxt and c == MT1:
                        items.append(("max1", 0))
                    if nxt:
                        items += [("score", 2 * c), ("score", 2 * c + 1)]
                    if prev and c == OT0:
                        items += [("out0", t) for t in range(0, 4, OT_TILES)]
                    if cur and c == OT1:
                        items += [("out1", t) for t in range(0, 4, OT_TILES)]
                    slots_.append([(what, i, place + n) for n, (what, i) in enumerate(items)])
                    place += len(items)
                return slots_

            def uses(where):
                return sum(len(items) for items in ring_items(where))

            def place_of(where, what, i=0):
                return [p for items in ring_items(where) for w, j, p in items if (w, j) == (what, i)][0]

            WHERE = ("before", "first") + ("inner",) * (PAIRS - 2) + ("last", "after")

            def ring_base(u):
                return sum(uses(WHERE[i]) for i in range(u + 1))

            def ring_bank(item):
                return bank(RING_BANKS[item % RING])

            def chunk_bank(item):
                return bank(3 + item % ST_RING)

            def walk(step):
                for u in range(-1, PAIRS + 1):
                    step(u, u % 2, WHERE[u + 1])

            def no_side(tick):
                pass

            with nc.Block() as block:
                @block.sync
                def _(sp):
                    clear(sp, clears)

                    def head_rows(rows_, head):
                        return rows_[2 * kind + w, :, bass.ds(head * HD, HD), :]

                    def load_queries(dst, u, par, signal):
                        for h in range(2):
                            sp.dma_start(dst[HROWS * h:HROWS * (h + 1), par, h, :], head_rows(q_rows, 2 * u + h))\
                                .then_inc(signal, 16)

                    def load_keys(dst, u, par, signal):
                        for h in range(2):
                            sp.dma_start(dst[HROWS * h:HROWS * (h + 1), par, :], head_rows(k_rows, 2 * u + h))\
                                .then_inc(signal, 16)

                    def load_pass_one(u, par, wait):
                        if wait:
                            sp.wait_ge(s["max_ready"], 2 * (u - 1))
                        load_queries(QM, u, par, m_loaded[par])
                        load_keys(KM, u, par, m_loaded[par])

                    def load_pass_two(u, par, wait):
                        if wait:
                            sp.wait_ge(s["exp_done"], (u - 1) * 2 * NC)
                        load_queries(QS, u, par, s_loaded[par])
                        load_keys(KS, u, par, s_loaded[par])

                    def max_rows(u, par, half):
                        step_, what = (u, "max0") if half == 0 else (u - 1, "max1")
                        sp.wait_ge(s["ring_free"], ring_base(step_) + place_of(WHERE[step_ + 1], what) + 1)
                        sp.wait_ge(s_loaded[par], loads(u, par))
                        for h in range(2):
                            r = HROWS * h + MAX_ROW
                            sp.dma_start(QS[r:r + 2, par, h, half * HALF:(half + 1) * HALF],
                                         maxT[8 * h:8 * h + 8, half, :]).then_inc(max_sent[half], 16)

                    run_side = beside(side.sync(sp)) if side else no_side
                    if fresh:
                        sp.wait_ge(SPROJ["written"], 16 * 6)
                    load_pass_one(0, 0, False)
                    if fresh:
                        for part in range(3):
                            write_parts(sp, kind, w, part, EARLY, D, SPROJ["written_rest"])
                    load_pass_two(0, 0, False)
                    load_pass_one(1, 1, False)
                    run_side(0)
                    if fresh:
                        sp.wait_ge(SPROJ["written_rest"], 16 * 6)
                    max_rows(0, 0, 1)
                    for u in range(PAIRS):
                        tick = (u + 1) * NC
                        if u + 1 < PAIRS:
                            load_pass_two(u + 1, (u + 1) % 2, u > 0)
                        if u + 2 < PAIRS:
                            load_pass_one(u + 2, u % 2, True)
                        run_side(tick + 1)
                        max_rows(u, u % 2, 0)
                        run_side(tick + MT0 + 1)
                        if u + 1 < PAIRS:
                            max_rows(u + 1, (u + 1) % 2, 1)
                        run_side(tick + MT1 + 1)
                    run_side(float("inf"))
                    for half in range(2):
                        sp.wait_ge(max_sent[half], 32 * PAIRS)

                @block.gpsimd
                def _(g):

                    def stage_values(u, par, wait):
                        if wait:
                            g.wait_ge(s["pv_done"], (u - 1) * NG)
                        nc.gpsimd.tensor_copy(v_pair[:, par], v_aug[:, :, bass.ds(2 * u, 2), :]).then_inc(s["v_staged"], 1)

                    def split_max(w, half):
                        i = 2 * w + (1 - half)
                        g.wait_ge(s["max_found"], i + 1)
                        nm = neg_max[:, half].rearrange("p t h -> p h t")
                        nc.gpsimd.tensor_copy(max_bf[:, half, :, 0, :], nm).then_inc(s["max_step"], 1)
                        g.wait_ge(s["max_step"], i + 1)
                        nc.gpsimd.tensor_tensor(max_bf[:, half, :, 1, :], nm, max_bf[:, half, :, 0, :],
                                                ALU.subtract).then_inc(s["max_ready"], 1)

                    def normalise(w, half, step_, where):
                        e = 2 * w + (1 - half)
                        place = place_of(where, "out0" if half == 0 else "out1", 4 - OT_TILES)
                        g.wait_ge(s["ring_free"], ring_base(step_) + place + 1)
                        nc.gpsimd.tensor_tensor(o_sum[:, half], o_turned[:, half, :, :, 0], o_turned[:, half, :, :, 1],
                                                ALU.add).then_inc(s["o_step"], 1)
                        g.wait_ge(s["o_step"], 2 * e + 1)
                        nc.gpsimd.tensor_tensor(o_rec[:, half], o_sum[:, half, :, :, HD], minus_one[:, :, :],
                                                ALU.pow).then_inc(s["o_step"], 1)
                        g.wait_ge(s["o_step"], 2 * e + 2)
                        nc.gpsimd.tensor_tensor(
                            attn[:, 4 * half:4 * half + 4, bass.ds(2 * HD * w, 2 * HD)]
                            .rearrange("p t (h d) -> p t h d", h=2),
                            o_sum[:, half, :, :, 0:HD],
                            o_rec[:, half].unsqueeze(3).broadcast_to([P, 4, 2, HD]), ALU.mult)\
                            .then_inc(s["normed"], 1)

                    run_side = beside(side.gpsimd(g)) if side else no_side

                    def step(u, par, where):
                        cur, nxt, prev = flags(where)
                        tick = (u + 1) * NC
                        if nxt:
                            stage_values(u + 1, 1 - par, prev)
                        run_side(tick + 1)
                        if prev:
                            normalise(u - 1, 0, u, where)
                        run_side(tick + OT0 + 1)
                        if nxt:
                            split_max(u + 1, 1)
                        run_side(tick + QT)
                        if nxt:
                            split_max(u + 1, 0)
                        if cur:
                            normalise(u, 1, u, where)
                        run_side(tick + NC)
                    walk(step)
                    run_side(float("inf"))

                @block.tensor
                def _(pe):
                    run_side = beside(side.tensor(pe)) if side else no_side

                    def step(u, par, where):
                        cur, nxt, prev = flags(where)
                        base = ring_base(u)

                        def ring(place):
                            if base + place >= RING:
                                pe.wait_ge(s["ring_free"], base + place - RING + 1)
                            return ring_bank(base + place)

                        def values(v, vpar, i):
                            half, j, _ = chunk(2 * i)
                            first, last = j == 0, j + 2 == HALF_TILES[1 - half]
                            pe.wait_ge(s["exp_done"], 2 * (v * NC + 2 * i + 2))
                            if first and half == 1:
                                pe.wait_ge(s["v_staged"], v + 1)
                                if v > 0:
                                    pe.wait_ge(s["o_evac"], 2 * v)
                            if first and half == 0:
                                pe.wait_ge(s["o_evac"], 2 * v + 1)
                            for h in range(2):
                                if first and not full and half == 0:
                                    nc.tensor.matmul(bank(6)[64 * h + 32:64 * h + 32 + HD + 1, 0:P],
                                                     v_pair[:, vpar, 1, h, :], zeros[:, :], start=True, stop=False,
                                                     skip_group_check=True)
                            for odd in range(2):
                                _, jj, c0 = chunk(2 * i + odd)
                                for h in range(2):
                                    r = 64 * h + 32 * odd
                                    mm = nc.tensor.matmul(
                                        bank(6)[r:r + HD + 1, c0:HALF], v_pair[:, vpar, jj, h, :],
                                        probs[:, (2 * i + odd) % 4, h, c0:HALF],
                                        start=first and c0 == 0, stop=last, skip_group_check=True)
                            mm.then_inc(s["pv_done"], 1)

                        def turn_out(v, half, tile, place):
                            e = 2 * v + (1 - half)
                            dst = ring(place)
                            pe.wait_ge(s["o_evac"], e + 1)
                            for t in range(tile, tile + OT_TILES):
                                mm = nc.tensor.transpose(dst[:, t * P:(t + 1) * P],
                                                         o_sb[:, 1 - half, t * P:(t + 1) * P], ident[:, :])
                            mm.then_inc(s["ring_full"], 1)

                        def turn_max(v, half, place):
                            dst = ring(place)
                            pe.wait_ge(s["max_ready"], 2 * v + (1 - half) + 1)
                            nc.tensor.transpose(dst[0:16, 0:P // 2].bitcast(BF16),
                                                max_bf[:, half].rearrange("p h l t -> p (h l t)"),
                                                identb[:, :]).then_inc(s["ring_full"], 1)

                        for c, items in enumerate(ring_items(where)):
                            def scores(i, place):
                                half, r, h, kb, n = score(i)
                                if i == 0:
                                    pe.wait_ge(m_loaded[1 - par], loads(u + 1, 1 - par))
                                dst = ring(place)
                                qt = 4 * half + r
                                nc.tensor.matmul(dst[:, 0:n], QM[:, 1 - par, h, qt * P:(qt + 1) * P],
                                                 KM[:, 1 - par, kb * HALF:kb * HALF + n],
                                                 start=True, stop=True).then_inc(s["ring_full"], 1)

                            def chunk_scores(h):
                                half, j, c0 = chunk(c)
                                if h == 0 and (c == 0 or c == QT):
                                    pe.wait_ge(s_loaded[par], loads(u, par))
                                    pe.wait_ge(max_sent[half], 32 * u + 32)
                                item = 2 * (u * NC + c) + h
                                if item >= ST_RING:
                                    pe.wait_ge(s["exp_done"], item - ST_RING + 1)
                                dst = chunk_bank(item)
                                mm = nc.tensor.matmul(dst[:, c0:HALF], KS[:, par, j * P:(j + 1) * P],
                                                      QS[:, par, h, half * HALF + c0:(half + 1) * HALF],
                                                      start=True, stop=c not in DIAG)
                                if c in DIAG:
                                    mm = nc.tensor.matmul(dst[:, c0:c0 + P], identb[:, :], later[:, :],
                                                          start=False, stop=True)
                                mm.then_inc(s["st_full"], 1)

                            for what, i, place in items:
                                if what == "score" and i % 2 == 0:
                                    scores(i, place)
                                if what == "max0":
                                    turn_max(u, 0, place)
                                if what == "max1":
                                    turn_max(u + 1, 1, place)
                            if cur:
                                chunk_scores(0)
                            for what, i, place in items:
                                if what == "score" and i % 2 == 1:
                                    scores(i, place)
                            if cur:
                                chunk_scores(1)
                            if prev and c == 1:
                                values(u - 1, 1 - par, NG - 1)
                            if cur and c >= 3 and c % 2 == 1:
                                values(u, par, (c - 3) // 2)
                            for what, i, place in items:
                                if what == "out0":
                                    turn_out(u - 1, 0, i, place)
                                if what == "out1":
                                    turn_out(u, 1, i, place)
                            run_side((u + 1) * NC + c)
                    walk(step)
                    run_side(float("inf"))

                @block.scalar
                def _(a):

                    def evacuate(v, half, groups, wait):
                        e = 2 * v + (1 - half)
                        a.wait_ge(s["pv_done"], groups)
                        if wait:
                            a.wait_ge(s["normed"], e - half)
                        nc.scalar.activation(o_sb[:, 1 - half, :], bank(6), ACT.Identity).then_inc(s["o_evac"], 1)

                    run_side = beside(side.scalar(a)) if side else no_side

                    def step(u, par, where):
                        cur, nxt, prev = flags(where)
                        for c in range(NC):
                            if cur:
                                half, j, c0 = chunk(c)
                                if u > 0 or c >= 4:
                                    a.wait_ge(s["pv_done"], u * NG + c // 2 - 1)
                                for h in range(2):
                                    item = 2 * (u * NC + c) + h
                                    a.wait_ge(s["st_full"], item + 1)
                                    nc.scalar.activation(probs[:, c % 4, h, c0:HALF], chunk_bank(item)[:, c0:HALF],
                                                         ACT.Exp).then_inc(s["exp_done"], 1)
                            if prev and c == 1:
                                evacuate(u - 1, 0, u * NG, True)
                            if cur and c == 9:
                                evacuate(u, 1, u * NG + 4, u > 0)
                            run_side((u + 1) * NC + c)
                    walk(step)
                    run_side(float("inf"))

                @block.vector
                def _(v):

                    run_side = beside(side.vector(v)) if side else no_side

                    def step(u, par, where):
                        base = ring_base(u)

                        def full_bank(place):
                            v.wait_ge(s["ring_full"], base + place + 1)
                            return ring_bank(base + place)

                        def find_max(half, place):
                            v.wait_ge(s["ring_free"], base + place + 1)
                            nb = 2 if full or half == 1 else 1
                            nc.vector.tensor_reduce(neg_max[:, half], parts[:, half, :, :, 0:nb], op=ALU.max,
                                                    axis=AX.X, negate=True).then_inc(s["max_found"], 1)

                        def copy_max(w, half, place):
                            src = full_bank(place)
                            if where in ("inner", "last") or (where == "first" and half == 1):
                                v.wait_ge(max_sent[half], 32 * w)
                            nc.vector.tensor_copy(maxT[:, half, :], src[0:16, 0:P // 2].bitcast(BF16))\
                                .then_inc(s["ring_free"], 1)

                        def copy_out(w, half, tile, place):
                            src = full_bank(place).rearrange("p (t h g c) -> p t h g c", t=4, h=2, g=2)
                            if where != "first":
                                v.wait_ge(s["normed"], 2 * w + 1 - half)
                            ts = slice(tile, tile + OT_TILES)
                            nc.vector.tensor_copy(o_turned[:, half, ts].rearrange("p t h g c -> p t (h g) c"),
                                                  src[:, ts, :, :, 0:HD + 1].rearrange("p t h g c -> p t (h g) c"))\
                                .then_inc(s["ring_free"], 1)

                        for c, items in enumerate(ring_items(where)):
                            for what, i, place in items:
                                if what == "score":
                                    half, r, h, kb, n = score(i)
                                    dst = parts[:, half, r, h, kb:kb + 1]
                                    if full or kb != half:
                                        src = full_bank(place)
                                        nc.vector.tensor_reduce(dst, src, op=ALU.max, axis=AX.X)\
                                            .then_inc(s["ring_free"], 1)
                                    else:
                                        src = full_bank(place)
                                        nc.vector.tensor_tensor_reduce(
                                            out=masked_out[:, i % 4, 0:n], in0=src[:, 0:n],
                                            in1=causal[:, 4 * P - n:4 * P], scale=1.0, scalar=LOWEST,
                                            op0=ALU.add, op1=ALU.max, accum_out=dst).then_inc(s["ring_free"], 1)
                                    if i == 15:
                                        find_max(1, place)
                                    if i == NS - 1:
                                        find_max(0, place)
                                if what == "max0":
                                    copy_max(u, 0, place)
                                if what == "max1":
                                    copy_max(u + 1, 1, place)
                                if what == "out0":
                                    copy_out(u - 1, 0, i, place)
                                if what == "out1":
                                    copy_out(u, 1, i, place)
                            run_side((u + 1) * NC + c)
                    walk(step)
                    run_side(float("inf"))

        def turned_half(a, turned, signal, dst, b0, h, scale=1.0, bias=0.0):
            a.wait_ge(turned, 4 * (h + 1))
            nc.scalar.activation(dst[:, h * HALF:(h + 1) * HALF], bank(b0 + h), ACT.Identity, bias=bias,
                                 scale=scale).then_inc(signal, 1)

        def token_rows(t):
            return slice((t % 4) * P, (t % 4 + 1) * P)

        def tokens(b_):
            return b_.rearrange("p (t d) -> p t d", t=4)

        def over_tiles(row, n):
            return row.unsqueeze(1).broadcast_to([P, n, row.shape[-1]])

        def output_projection(s, w, w_out, bias_row):
            x, attn = xs[w], attns[w]

            def tensor(pe):
                turn_tensor(pe, None, s["attn_turned"], attn, 0)
                for t in range(QT):
                    if t % 4 == 0:
                        pe.wait_ge(s["attnT"], t // 4 + 1)
                    nc.tensor.matmul(bank(2 + t // 4)[:, token_rows(t)], xnT[:, t * P:(t + 1) * P], w_out[:, :],
                                     start=True, stop=True).then_inc(s["proj"], 1)

            def scalar(a):
                for h in range(2):
                    turned_half(a, s["attn_turned"], s["attnT"], xnT, 0, h)

            def gpsimd(g):
                nc.gpsimd.tensor_tensor(xb[:, :, :], x[:, :, :], over_tiles(bias_row, QT), ALU.add)\
                    .then_inc(s["bias"], 1)

            def vector(v):
                v.wait_ge(s["bias"], 1)
                for h in range(2):
                    v.wait_ge(s["proj"], 4 * (h + 1))
                    nc.vector.tensor_tensor(x[:, 4 * h:4 * h + 4, :], xb[:, 4 * h:4 * h + 4, :],
                                            tokens(bank(2 + h)), ALU.add).then_inc(s["resid"], 1)
                v.wait_ge(s["resid"], 2)
            return tensor, scalar, gpsimd, vector

        def residual_stage(seq, w, clears):
            x, attn = xs[w], attns[w]
            with nc.Block() as block:
                @block.sync
                def _(sp):
                    clear(sp, clears)
                    sp.dma_start(attn[:, :, :], x_in[seq]).then_inc(SR["x0"], 16)

                @block.gpsimd
                def _(g):
                    layer_norm_pool(g, SR)
                    g.wait_ge(SR["x0"], 16)
                    nc.gpsimd.tensor_tensor(xb[:, :, :], attn[:, :, :], over_tiles(trows[:, FIN_B, :], QT), ALU.add)\
                        .then_inc(SR["normed"], 1)
                    layer_norm_pool(g, SR2)

                @block.vector
                def _(v):
                    layer_norm_vector(v, SR, x, xhat)
                    v.wait_ge(SR["xhat"], QT)
                    nc.vector.tensor_tensor(xhat[:, :, :], xhat[:, :, :], over_tiles(trows[:, FIN_W, :], QT),
                                            ALU.mult).then_inc(SR["scaled"], 1)
                    v.wait_ge(SR["scaled"], 1)
                    v.wait_ge(SR["normed"], 1)
                    nc.vector.tensor_tensor(x[:, :, :], xhat[:, :, :], xb[:, :, :], ALU.add).then_inc(SR["sum"], 1)
                    v.wait_ge(SR["sum"], 1)
                    layer_norm_vector(v, SR2, x, x)

        def ternary_stage(w, clears):
            x = xs[w]
            s = ST

            def hidden_layer(pe, w, src, signal, ready):
                pe.wait_ge(ready, 2 * FT)
                for n in range(2 * FT):
                    h, f = n // FT, n % FT
                    for i in range(FT):
                        mm = nc.tensor.matmul(bank(n), w[:, i, f * P:(f + 1) * P], src[:, i, h * HALF:(h + 1) * HALF],
                                              start=i == 0, stop=i == FT - 1)
                    mm.then_inc(signal, 1)

            with nc.Block() as block:
                @block.sync
                def _(sp):
                    clear(sp, clears)

                @block.gpsimd
                def _(g):
                    layer_norm_pool(g, s)

                @block.tensor
                def _(pe):
                    turn_tensor(pe, None, s["turned"], x, 0)
                    for n in range(2 * FT):
                        h, f = n // FT, n % FT
                        pe.wait_ge(s["xnT"], h + 1)
                        if n >= 3:
                            pe.wait_ge(s["hidden"], n - 2)
                        for i, (w, signal) in enumerate(((tw1, s["gate"]), (tw2, s["up"]))):
                            nc.tensor.matmul(bank(2 + 2 * (n % 3) + i), w[:, f * P:(f + 1) * P],
                                             xnT[:, h * HALF:(h + 1) * HALF], start=True, stop=True)\
                                .then_inc(signal, 1)
                    hidden_layer(pe, th1, hidB, s["h1"], s["hidden"])
                    hidden_layer(pe, th2, hidA, s["h2"], s["g1"])
                    pe.wait_ge(s["g2"], 2 * FT)
                    for t in range(QT):
                        for f in range(FT):
                            mm = nc.tensor.matmul(bank(t // 4)[:, token_rows(t)], hidB[:, f, t * P:(t + 1) * P],
                                                  tw3[:, f, :], start=f == 0, stop=f == FT - 1)
                        mm.then_inc(s["w3"], 1)

                @block.scalar
                def _(a):
                    for h in range(2):
                        turned_half(a, s["turned"], s["xnT"], xnT, 0, h)
                    for n in range(2 * FT):
                        h, f = n // FT, n % FT
                        a.wait_ge(s["gate"], n + 1)
                        nc.scalar.activation(hidA[:, f, h * HALF:(h + 1) * HALF], bank(2 + 2 * (n % 3)), ACT.Silu,
                                             scale=tcols[:, S_W1 + f:S_W1 + f + 1]).then_inc(s["silu"], 1)
                    for ready, signal, dst, col in ((s["h1"], s["g1"], hidA, S_H1), (s["h2"], s["g2"], hidB, S_H2)):
                        for n in range(2 * FT):
                            h, f = n // FT, n % FT
                            a.wait_ge(ready, n + 1)
                            nc.scalar.activation(dst[:, f, h * HALF:(h + 1) * HALF], bank(n), ACT.Gelu,
                                                 scale=tcols[:, col + f:col + f + 1]).then_inc(signal, 1)

                @block.vector
                def _(v):
                    for n in range(2 * FT):
                        h, f = n // FT, n % FT
                        v.wait_ge(s["up"], n + 1)
                        v.wait_ge(s["silu"], n + 1)
                        hs = slice(h * HALF, (h + 1) * HALF)
                        nc.vector.scalar_tensor_tensor(out=hidB[:, f, hs], in0=bank(3 + 2 * (n % 3)),
                                                       scalar=tcols[:, S_W2 + f:S_W2 + f + 1], in1=hidA[:, f, hs],
                                                       op0=ALU.mult, op1=ALU.mult).then_inc(s["hidden"], 1)
                    for h in range(2):
                        v.wait_ge(s["w3"], 4 * (h + 1))
                        nc.vector.tensor_tensor(xb[:, 4 * h:4 * h + 4, :], tokens(bank(h)),
                                                over_tiles(trows[:, S_W3, :], 4), ALU.mult).then_inc(s["scaled"], 1)
                    v.wait_ge(s["scaled"], 2)
                    nc.vector.tensor_tensor(x[:, :, :], x[:, :, :], xb[:, :, :], ALU.add).then_inc(s["sum"], 1)
                    v.wait_ge(s["sum"], 1)
                    layer_norm_vector(v, s, x, x)

        def differential_stage(w, clears):
            s, x, attn = SF, xs[w], attns[w]
            proj_tensor, proj_scalar, proj_gpsimd, proj_vector = output_projection(s, w, dwo, trows[:, T_BP, :])
            with nc.Block() as block:
                @block.sync
                def _(sp):
                    clear(sp, clears)

                @block.gpsimd
                def _(g):
                    proj_gpsimd(g)
                    layer_norm_pool(g, s)

                @block.vector
                def _(v):
                    nc.vector.scalar_tensor_tensor(out=attn[:, :, 0:D // 2], in0=attn[:, :, D // 2:D],
                                                   scalar=lam_mean[:, 3:4], in1=attn[:, :, 0:D // 2],
                                                   op0=ALU.mult, op1=ALU.add).then_inc(s["mixed"], 1)
                    proj_vector(v)
                    layer_norm_vector(v, s, x, x)

                @block.scalar
                def _(a):
                    proj_scalar(a)

                @block.tensor
                def _(pe):
                    pe.wait_ge(s["mixed"], 1)
                    proj_tensor(pe)

        def experts_stage(seq, w, clears):
            s, x = SM, xs[w]
            loaded = (s["loaded0"], s["loaded1"])
            with nc.Block() as block:
                @block.sync
                def _(sp):
                    clear(sp, clears)

                    def load(e, par, wait):
                        if wait:
                            wait_alone(sp, s["y"], 2 * (e - 1))
                        sp.dma_start(ew1[:, par, :], moe_w1[e]).then_inc(loaded[par], 16)
                        sp.dma_start(ew2[:, par, :, :], moe_w2[e]).then_inc(loaded[par], 16)
                    load(0, 0, False)
                    load(1, 1, False)
                    with sp.Fori(2, EXPERTS - 1, 2) as e:
                        load(e, 0, True)
                        load(e + 1, 1, True)
                    sp.wait_ge(s["xhat"], QT)
                    sp.dma_start(out[seq], x[:, :, :]).then_inc(s["stored"], 16)
                    sp.wait_ge(s["stored"], 16)

                @block.gpsimd
                def _(g):
                    layer_norm_pool(g, s)

                @block.tensor
                def _(pe):
                    turn_tensor(pe, None, s["turned"], x, 0)
                    pe.wait_ge(s["xnT"], 2)
                    for t in range(QT):
                        mm = nc.tensor.matmul(bank(1)[:, t * EXPERTS:(t + 1) * EXPERTS], xnT[:, t * P:(t + 1) * P],
                                              sw[:, :], start=True, stop=True)
                    mm.then_inc(s["logits"], 1)

                    def expert(e, par, first, second=False):
                        hid = (hidA, hidB)[par]
                        pe.wait_ge(loaded[par], 16 * e + 32 - 16 * par)
                        for n in range(2 * FT):
                            h, f = n // FT, n % FT
                            if not first or n >= 4:
                                pe.wait_ge(s["gelu"], 2 * FT * e + n - 3)
                            nc.tensor.matmul(bank(2 + n % 4), ew1[:, par, f * P:(f + 1) * P],
                                             xnT[:, h * HALF:(h + 1) * HALF], start=True, stop=True)\
                                .then_inc(s["hidden"], 1)
                        for h in range(2):
                            pe.wait_ge(s["gelu"], 2 * FT * e + FT * (h + 1))
                            if not first:
                                pe.wait_ge(s["tmp"], 2 * e - 1 + h)
                            for t in range(4 * h, 4 * h + 4):
                                for f in range(FT):
                                    mm = nc.tensor.matmul(bank(6 + h)[:, token_rows(t)], hid[:, f, t * P:(t + 1) * P],
                                                          ew2[:, par, f, :], start=f == 0, stop=f == FT - 1)
                            mm.then_inc(s["y"], 1)
                    expert(0, 0, True)
                    expert(1, 1, False)
                    with pe.Fori(2, EXPERTS - 1, 2) as e:
                        expert(e, 0, False)
                        expert(e + 1, 1, False)

                @block.scalar
                def _(a):
                    for h in range(2):
                        turned_half(a, s["turned"], s["xnT"], xnT, 0, h)
                    a.wait_ge(s["step"], 3)
                    nc.scalar.activation(lexp[:, :, :], logit[:, :, :], ACT.Exp).then_inc(s["lexp"], 1)

                    def expert(e, par, wait):
                        hid = (hidA, hidB)[par]
                        for n in range(2 * FT):
                            h, f = n // FT, n % FT
                            if wait and n == 0:
                                wait_alone(a, s["y"], 2 * e - 2)
                            wait_alone(a, s["hidden"], 2 * FT * e + n + 1)
                            nc.scalar.activation(hid[:, f, h * HALF:(h + 1) * HALF], bank(2 + n % 4),
                                                 ACT.Gelu_apprx_tanh, bias=eb1[:, e, f:f + 1]).then_inc(s["gelu"], 1)
                    expert(0, 0, False)
                    expert(1, 1, False)
                    with a.Fori(2, EXPERTS - 1, 2) as e:
                        expert(e, 0, True)
                        expert(e + 1, 1, True)

                @block.vector
                def _(v):
                    step = [0]

                    def then(ins):
                        step[0] += 1
                        ins.then_inc(s["step"], 1)
                        v.wait_ge(s["step"], step[0])

                    def per_token(a_):
                        return a_.unsqueeze(2).broadcast_to([P, QT, EXPERTS])

                    v.wait_ge(s["logits"], 1)
                    logits = bank(1)[:, 0:QT * EXPERTS].rearrange("p (t e) -> p t e", e=EXPERTS)
                    then(nc.vector.tensor_tensor(logit[:, :, :], logits, over_tiles(swb[:, :], QT), ALU.add))
                    then(nc.vector.tensor_reduce(lmax[:, :], logit[:, :, :], op=ALU.max, axis=AX.X))
                    then(nc.vector.tensor_tensor(logit[:, :, :], logit[:, :, :], per_token(lmax[:, :]), ALU.subtract))
                    v.wait_ge(s["lexp"], 1)
                    then(nc.vector.tensor_reduce(lsum[:, :], lexp[:, :, :], op=ALU.add, axis=AX.X))
                    then(nc.vector.reciprocal(lsum[:, :], lsum[:, :]))
                    then(nc.vector.tensor_tensor(prob[:, :, :], lexp[:, :, :], per_token(lsum[:, :]), ALU.mult))
                    then(nc.vector.tensor_reduce(lmax[:, :], prob[:, :, :], op=ALU.max, axis=AX.X))
                    then(nc.vector.tensor_tensor(gate[:, :, :], prob[:, :, :], per_token(lmax[:, :]), ALU.is_equal))
                    then(nc.vector.tensor_tensor(gate[:, :, :], gate[:, :, :], over_tiles(rank[:, :], QT), ALU.mult))
                    then(nc.vector.tensor_reduce(lsum[:, :], gate[:, :, :], op=ALU.max, axis=AX.X))
                    then(nc.vector.tensor_tensor(gate[:, :, :], gate[:, :, :], per_token(lsum[:, :]), ALU.is_equal))
                    then(nc.vector.tensor_tensor(gate[:, :, :], gate[:, :, :], per_token(lmax[:, :]), ALU.mult))

                    def expert(e, first):
                        for h in range(2):
                            v.wait_ge(s["y"], 2 * e + h + 1)
                            if not first:
                                v.wait_ge(s["acc"], QT * e - 4 + 4 * h)
                            nc.vector.tensor_tensor(xhat[:, 4 * h:4 * h + 4, :], tokens(bank(6 + h)),
                                                    over_tiles(eb2[:, e, :], 4), ALU.add).then_inc(s["tmp"], 1)
                            v.wait_ge(s["tmp"], 2 * e + h + 1)
                            for t in range(4 * h, 4 * h + 4):
                                nc.vector.scalar_tensor_tensor(out=x[:, t, :], in0=xhat[:, t, :],
                                                               scalar=gate[:, t, bass.ds(e, 1)], in1=x[:, t, :],
                                                               op0=ALU.mult, op1=ALU.add).then_inc(s["acc"], 1)
                    expert(0, True)
                    with v.Fori(1, EXPERTS) as e:
                        expert(e, False)
                    v.wait_ge(s["acc"], QT * EXPERTS)
                    layer_norm_vector(v, s, x, x)

        X, Y = 0, 1
        with nc.Fori(0, B - 1, 2) as b:
            with nc.Block() as block:
                @block.sync
                def _(sp):
                    clear(sp, (S0, SM))
                    for w in range(2):
                        sp.dma_start(xs[w][:, :, :], x_in[b + w]).then_inc(SL["x"], 16)
                    sp.wait_ge(SL["x"], 32)
            project_stage(0, X, [SL])
            attention_stage(0, X, [], True, Side(Y, 0, False, True, False, 2, 1.5, (SPROJ["written_rest"], 16 * 6)))
            with nc.Fori(0, LAYERS - 1) as l:
                attention_stage(0, Y, [SPROJ, SATT[X], SIDE[Y]], False, Side(X, l, True, True, True, 3, 2))
                attention_stage(0, X, [SATT[Y], SIDE[X]], False, Side(Y, l, True, True, False, 3, 2))
            attention_stage(0, Y, [SATT[X], SIDE[Y]], False, Side(X, LAYERS - 1, True, False, True, 3, 2))
            residual_stage(b, X, [SATT[Y], SIDE[X]])
            ternary_stage(X, [SR, SR2])
            project_stage(1, X, [ST])
            attention_stage(1, X, [], True, Side(Y, LAYERS - 1, True, False, False, 3, 2))
            residual_stage(b + 1, Y, [SPROJ, SATT[X], SIDE[Y]])
            ternary_stage(Y, [SR, SR2])
            project_stage(1, Y, [ST])
            attention_stage(1, Y, [], True)
            differential_stage(X, [SPROJ, SATT[Y]])
            experts_stage(b, X, [SF])
            differential_stage(Y, [SM])
            experts_stage(b + 1, Y, [SF])


def kernel(**inputs):
    import concourse.bacc as bacc
    from concourse.bass_utils import run_bass_kernel_spmd
    import ml_dtypes
    bf16 = np.dtype(ml_dtypes.bfloat16)
    g = {k: np.asarray(v) for k, v in inputs.items()}

    def a(name):
        return g["L0_attn_" + name]

    def columns(v):
        return v.reshape(-1, P).T

    def spread(v):
        return np.broadcast_to(v[None], (P,) + v.shape)

    def tiles(w):
        return w.reshape(-1, P, w.shape[-1]).transpose(1, 0, 2)

    def blocks(rows):
        lead = rows.shape[:-3]
        return np.moveaxis(rows.reshape(lead + (HEADS, -1, HD, T)), -3, -4).reshape(lead + (-1, D, T))

    layer_cols = np.stack([np.concatenate([
        columns(a("ln1_w")[i]), columns(a("ln1_b")[i]), columns(a("ln2_w")[i]), columns(a("ln2_b")[i]),
        columns(a("in_proj_b")[i, 0:D]), columns(a("in_proj_b")[i, D:2 * D]), columns(a("ffn1_b")[i])], 1)
        for i in range(LAYERS)])
    layer_rows = np.stack([spread(np.stack([a("in_proj_b")[i, 2 * D:], a("out_proj_b")[i], a("ffn2_b")[i]]))
                           for i in range(LAYERS)])
    tail_cols = np.concatenate([columns(g["L0_ffn_" + n]) for n in ("w1_s", "w2_s", "h1_s", "h2_s")]
                               + [columns(g["L1_attn_bq"]), columns(g["L1_attn_bk"])], 1)
    tail_rows = spread(np.stack([a("final_w"), a("final_b"), g["L0_ffn_w3_s"], g["L1_attn_bv"], g["L1_attn_bp"]]))
    lambdas = spread(np.stack([g["L1_attn_lambda_" + n][:, 0, :] for n in ("q1", "k1", "q2", "k2")]))

    pos = np.arange(T)
    ident = np.eye(P, dtype=np.float32)
    causal = np.zeros((P, 4 * P), np.float32)
    causal[:, 3 * P:] = np.where(np.arange(P)[None, :] > np.arange(P)[:, None], MASKED, 0.0)
    later = np.where(np.arange(P)[:, None] > np.arange(P)[None, :], MASKED, 0.0).astype(bf16)
    slopes = ((2.0 ** -(2.0 ** -(np.log2(HEADS) - 3))) ** np.arange(1, HEADS + 1)).astype(np.float32)
    q_extra = np.zeros((2, HEADS, EXTRA_ROWS, T), bf16)
    rest = slopes.copy()
    for i in range(3):
        part = rest.astype(bf16)
        q_extra[0, :, 2 * i:2 * i + 2, :] = part[:, None, None]
        rest = rest - part.astype(np.float32)
    k_extra = np.zeros((HEADS, EXTRA_ROWS, T), bf16)
    for i in range(3):
        k_extra[:, 2 * i, :] = (pos // 256 * 256).astype(bf16)
        k_extra[:, 2 * i + 1, :] = (pos % 256).astype(bf16)
    k_extra[:, 6:8, :] = 1.0

    arrays = {
        "x": g["L0_attn_x"].reshape(B, QT, P, D).transpose(0, 2, 1, 3),
        "layer_wi": a("in_proj_w").transpose(0, 2, 1),
        "layer_wo": a("out_proj_w").transpose(0, 2, 1),
        "layer_f1": a("ffn1_w").transpose(0, 2, 1),
        "layer_f2": np.stack([tiles(a("ffn2_w")[i].T) for i in range(LAYERS)]),
        "layer_cols": layer_cols, "layer_rows": layer_rows,
        "tern_w1": g["L0_ffn_w1_w"].T, "tern_w2": g["L0_ffn_w2_w"].T,
        "tern_h1": tiles(g["L0_ffn_h1_w"].T), "tern_h2": tiles(g["L0_ffn_h2_w"].T),
        "tern_w3": tiles(g["L0_ffn_w3_w"].T),
        "tail_cols": tail_cols, "tail_rows": tail_rows,
        "diff_w": np.concatenate([g["L1_attn_Wq"].T, g["L1_attn_Wk"].T, g["L1_attn_Wv"].T], 1),
        "diff_wp": g["L1_attn_Wp"].T, "lambdas": lambdas,
        "switch_w": g["L1_ffn_switch_w"], "switch_b": spread(g["L1_ffn_switch_b"]),
        "moe_w1": g["L1_ffn_w1"], "moe_b1": g["L1_ffn_b1"].reshape(EXPERTS, FT, P).transpose(2, 0, 1),
        "moe_w2": np.stack([tiles(g["L1_ffn_w2"][e]) for e in range(EXPERTS)]),
        "moe_b2": spread(g["L1_ffn_b2"]),
        "ident": ident, "identb": ident.astype(bf16), "causal": causal, "later": later,
        "q_extra": blocks(q_extra), "k_extra": blocks(k_extra),
    }
    nc = bacc.Bacc("TRN2", target_bir_lowering=False, num_devices=1)
    args = []
    for name in arrays:
        arrays[name] = np.ascontiguousarray(arrays[name])
        args.append(nc.dram_tensor("in_" + name, arrays[name].shape, mybir.dt.from_np(arrays[name].dtype),
                                   kind="ExternalInput").ap())
    out = nc.dram_tensor("out", (B, P, QT, D), F32, kind="ExternalOutput").ap()
    build(nc, *args, out)
    result = run_bass_kernel_spmd(nc, [{"in_" + k: v for k, v in arrays.items()}], core_ids=[0])
    return result.results[0]["out"].transpose(0, 2, 1, 3).reshape(B, T, D)
```

```python
import concourse.bass as bass
from concourse import mybir
from contextlib import ExitStack
import numpy as np

F32 = mybir.dt.float32
BF16 = mybir.dt.bfloat16
ALU = mybir.AluOpType
ACT = mybir.ActivationFunctionType
AX = mybir.AxisListType

P = 128
B, T, D = 4, 1024, 128
LAYERS = 4
HEADS, HD = 16, 8
PAIRS = HEADS // 2
FF = 512
FT = FF // P
EXPERTS = 8
QT = T // P
HALF = T // 2
EPS = 1e-5
SCALE = HD ** -0.5
LAMBDA_INIT = 0.8
X, Y = 0, 1

HROWS = 64
Q_PARTS = (0, 0, 0, 1, 2, 1)
K_PARTS = (1, 2, 0, 0, 0, 1)
PART_ROWS = len(Q_PARTS) * HD
ALIBI_ROW = PART_ROWS
MAX_ROW = ALIBI_ROW + 6
EXTRA_ROWS = HROWS - PART_ROWS
BLOCKS = HROWS // HD
EARLY = 4 * HD
MASKED = -1e30
LOWEST = -3e38

LN1_W, LN1_B, LN2_W, LN2_B, BQ, BK, B1 = 0, 1, 2, 3, 4, 5, 6
N_COLS = B1 + FT
BV, BO, B2 = 0, 1, 2
S_W1, S_W2, S_H1, S_H2, T_BQ, T_BK = 0, 4, 8, 12, 16, 17
N_TCOLS = 18
FIN_W, FIN_B, S_W3, T_BV, T_BP = range(5)


def build(nc, x_in, layer_wi, layer_wo, layer_f1, layer_f2, layer_cols, layer_rows,
          tern_w1, tern_w2, tern_h1, tern_h2, tern_w3, tail_cols, tail_rows,
          diff_w, diff_wp, lambdas, switch_w, switch_b, moe_w1, moe_b1, moe_w2, moe_b2,
          ident_in, identb_in, causal_in, later_in, q_extra, k_extra, out):
    ctx = ExitStack()
    with ctx:
        def sb(name, shape, dt=F32):
            return ctx.enter_context(nc.sbuf_tensor(name, shape, dt))

        ident = sb("ident", [P, P])
        identb = sb("identb", [P, P], BF16)
        causal = sb("causal", [P, 4 * P])
        later = sb("later", [P, P], BF16)
        zeros = sb("zeros", [P, P])
        neg_half = sb("neg_half", [P, QT])
        minus_one = sb("minus_one", [P, 4, 2])
        rank = sb("rank", [P, EXPERTS])
        wi = sb("wi", [P, 3 * D])
        wo = sb("wo", [P, D])
        f1 = sb("f1", [P, FF])
        f2 = sb("f2", [P, FT, D])
        cols = sb("cols", [P, N_COLS])
        rows = sb("rows", [P, 3, D])
        next_cols = sb("next_cols", [P, N_COLS])
        next_rows = sb("next_rows", [P, 3, D])
        tw1 = sb("tw1", [P, FF])
        tw2 = sb("tw2", [P, FF])
        th1 = sb("th1", [P, FT, FF])
        th2 = sb("th2", [P, FT, FF])
        tw3 = sb("tw3", [P, FT, D])
        tcols = sb("tcols", [P, N_TCOLS])
        trows = sb("trows", [P, 5, D])
        dwi = sb("dwi", [P, 3 * D])
        dwo = sb("dwo", [P, D])
        lam = sb("lam", [P, 4, HEADS // 2, HD])
        lam_work = sb("lam_work", [P, 2, HEADS // 2, HD])
        lam_sum = sb("lam_sum", [P, 2, HEADS // 2])
        lam_exp = sb("lam_exp", [P, 2, HEADS // 2])
        lam_mean = sb("lam_mean", [P, 4])
        sw = sb("sw", [P, EXPERTS])
        swb = sb("swb", [P, EXPERTS])
        ew1 = sb("ew1", [P, 2, FF])
        ew2 = sb("ew2", [P, 2, FT, D])
        eb1 = sb("eb1", [P, EXPERTS, FT])
        eb2 = sb("eb2", [P, EXPERTS, D])
        xs = [sb(f"x{w}", [P, QT, D]) for w in range(2)]
        xb = sb("xb", [P, QT, D])
        xhat = sb("xhat", [P, QT, D])
        xnT = sb("xnT", [P, T])
        stats = sb("stats", [P, QT, 6])
        mv = sb("mv", [P, QT, 2])
        var_eps = sb("var_eps", [P, QT])
        rstd = sb("rstd", [P, QT])
        v_augs = [sb(f"v_aug{w}", [P, QT, HEADS, HD + 1]) for w in range(2)]
        attns = [sb(f"attn{w}", [P, QT, D]) for w in range(2)]
        hidden = sb("hidden", [P, 8 * T])
        hidA = hidden[:, 0:FT * T].rearrange("p (f t) -> p f t", f=FT)
        hidB = hidden[:, FT * T:2 * FT * T].rearrange("p (f t) -> p f t", f=FT)
        q32, k32 = hidden[:, 0:T], hidden[:, T:2 * T]
        q_part = hidden[:, FT * T:FT * T + 3 * T // 2].bitcast(BF16).rearrange("p (n t) -> p n t", n=3)
        k_part = hidden[:, FT * T + 3 * T // 2:FT * T + 3 * T].bitcast(BF16).rearrange("p (n t) -> p n t", n=3)
        probs = sb("probs", [P, 4, 2, HALF])
        KM = sb("k_pass_one", [P, 2, T], BF16)
        KS = sb("k_pass_two", [P, 2, T], BF16)
        QM = sb("q_pass_one", [P, 2, 2, T], BF16)
        QS = sb("q_pass_two", [P, 2, 2, T], BF16)
        v_pair = sb("v_pair", [P, 2, QT, 2, HD + 1])
        o_sb = sb("o_sb", [P, 2, HALF])
        parts = sb("parts", [P, 2, 4, 2, 2])
        neg_max = sb("neg_max", [P, 2, 4, 2])
        max_bf = sb("max_bf", [P, 2, 2, 2, 4], BF16)
        maxT = sb("maxT", [16, 2, P], BF16)
        masked_out = sb("masked_out", [P, 4, 4 * P])
        o_turned = sb("o_turned", [P, 2, 4, 2, 2, HD + 1])
        o_sum = sb("o_sum", [P, 2, 4, 2, HD + 1])
        o_rec = sb("o_rec", [P, 2, 4, 2])
        logit = sb("logit", [P, QT, EXPERTS])
        lmax = sb("lmax", [P, QT])
        lexp = sb("lexp", [P, QT, EXPERTS])
        lsum = sb("lsum", [P, QT])
        prob = sb("prob", [P, QT, EXPERTS])
        gate = sb("gate", [P, QT, EXPERTS])

        psum = ctx.enter_context(nc.psum_tensor("psum", [P, 8 * 512], F32))

        def bank(i, n=1):
            return psum[:, i * 512:(i + n) * 512]

        q_rows = nc.dram_tensor("q_rows", (4, BLOCKS, D, T), BF16, kind="Internal").ap()
        k_rows = nc.dram_tensor("k_rows", (4, BLOCKS, D, T), BF16, kind="Internal").ap()

        def signals(stage, names):
            sems = {n: ctx.enter_context(nc.semaphore(f"{stage}_{n}")) for n in names.split()}
            return sems

        def clear(eng, stages):
            for stage in stages:
                for sem in stage.values():
                    eng.sem_clear(sem)

        waited = ctx.enter_context(nc.semaphore("waited"))
        LN = " stats moments var rstd xhat"
        SLATE = signals("late", "loaded written")
        S0 = signals("setup", "loaded memset lambda_step lambda_exp")
        SL = signals("load", "x y")
        ATT = ("load ring_full ring_free st_full exp_done pv_done v_staged o_evac o_step normed last_step"
               " max_ready max_step max_found m_loaded0 m_loaded1 s_loaded0 s_loaded1 max_rows0 max_rows1")
        SPROJ = signals("project", "loaded turned xnT qk v q32 k32 part1 rest part2 part3 v_ready written written_rest" + LN)
        SATT = [signals(f"attention{w}", ATT) for w in range(2)]
        SIDE = [signals(f"side{w}", "full free loaded prefetched x0 scaled sum bias bias2 gelu part1 rest part2 part3 written" + LN)
                for w in range(2)]
        SF = signals("differential", "mixed attn_turned attnT bias proj resid" + LN)
        ST = signals("tern", "turned xnT gate up silu hidden h1 g1 h2 g2 w3 scaled sum" + LN)
        SM = signals("moe", "turned xnT loaded0 loaded1 logits step gate hidden gelu y tmp acc stored lexp" + LN)

        def wait_alone(eng, sem, value):
            eng.wait_ge(sem, value)
            if not isinstance(value, int):
                eng.sem_inc(waited, 1)

        def layer_norm_vector(v, s, src, dst, norms=0):
            for t in range(QT):
                nc.vector.bn_stats(stats[:, t, :], src[:, t, :]).then_inc(s["stats"], 1)
            v.wait_ge(s["stats"], QT * (norms + 1))
            for t in range(QT):
                nc.vector.bn_aggr(mv[:, t, :], stats[:, t, :]).then_inc(s["moments"], 1)
            v.wait_ge(s["moments"], QT * (norms + 1))
            nc.vector.tensor_scalar(var_eps[:, :], mv[:, :, 1], EPS, None, ALU.add).then_inc(s["var"], 1)
            v.wait_ge(s["rstd"], norms + 1)
            for t in range(QT):
                nc.vector.tensor_scalar(dst[:, t, :], src[:, t, :], mv[:, t, 0:1], rstd[:, t:t + 1],
                                        ALU.subtract, ALU.mult).then_inc(s["xhat"], 1)

        def layer_norm_pool(g, s):
            g.wait_ge(s["var"], 1)
            nc.gpsimd.tensor_tensor(rstd[:, :], var_eps[:, :], neg_half[:, :], ALU.pow).then_inc(s["rstd"], 1)

        def turn_tensor(pe, ready, signal, src, b0):
            for t in range(QT):
                if ready is not None:
                    pe.wait_ge(ready, t + 1)
                nc.tensor.transpose(bank(b0 + t // 4)[:, (t % 4) * P:(t % 4 + 1) * P], src[:, t, :],
                                    ident[:, :]).then_inc(signal, 1)

        with nc.Block() as block:
            LOADS = [(ident, ident_in), (lam, lambdas), (identb, identb_in), (causal, causal_in), (later, later_in)]
            LATE = [(tw1, tern_w1), (tw2, tern_w2), (th1, tern_h1), (th2, tern_h2), (tw3, tern_w3),
                    (tcols, tail_cols), (sw, switch_w), (eb1, moe_b1), (dwi, diff_w), (dwo, diff_wp),
                    (trows, tail_rows), (swb, switch_b), (eb2, moe_b2)]

            @block.sync
            def _(sp):
                for dst, src in LOADS:
                    sp.dma_start(dst[:], src).then_inc(S0["loaded"], 16)
                for i in range(4):
                    sp.dma_start(q_rows[i, len(Q_PARTS):], q_extra[i // 2]).then_inc(SLATE["written"], 16)
                    sp.dma_start(k_rows[i, len(Q_PARTS):], k_extra).then_inc(SLATE["written"], 16)
                for dst, src in LATE:
                    sp.dma_start(dst[:], src).then_inc(SLATE["loaded"], 16)
                sp.wait_ge(S0["loaded"], 16 * len(LOADS))

            @block.gpsimd
            def _(g):
                nc.gpsimd.memset(QM[:], 0.0).then_inc(S0["memset"], 1)
                nc.gpsimd.memset(QS[:], 0.0).then_inc(S0["memset"], 1)
                nc.gpsimd.memset(zeros[:], 0.0).then_inc(S0["memset"], 1)
                nc.gpsimd.memset(minus_one[:], -1.0).then_inc(S0["memset"], 1)
                nc.gpsimd.memset(neg_half[:], -0.5).then_inc(S0["memset"], 1)
                for e in range(EXPERTS):
                    nc.gpsimd.memset(rank[:, e:e + 1], float(EXPERTS - e)).then_inc(S0["memset"], 1)
                for v_aug in v_augs:
                    nc.gpsimd.memset(v_aug[:, :, :, HD:HD + 1], 1.0).then_inc(S0["memset"], 1)

            @block.vector
            def _(v):
                v.wait_ge(S0["loaded"], 16 * len(LOADS))
                for i in range(2):
                    nc.vector.tensor_tensor(lam_work[:, i], lam[:, 2 * i], lam[:, 2 * i + 1],
                                            ALU.mult).then_inc(S0["lambda_step"], 1)
                v.wait_ge(S0["lambda_step"], 2)
                nc.vector.tensor_reduce(lam_sum[:, :, :], lam_work[:, :, :, :], op=ALU.add, axis=AX.X).then_inc(S0["lambda_step"], 1)
                v.wait_ge(S0["lambda_step"], 3)
                nc.vector.tensor_scalar(lam_sum[:, :, :], lam_sum[:, :, :], 5.0, None, ALU.min).then_inc(S0["lambda_step"], 1)
                v.wait_ge(S0["lambda_exp"], 1)
                nc.vector.tensor_reduce(lam_mean[:, 0:2], lam_exp[:, :, :], op=ALU.add, axis=AX.X).then_inc(S0["lambda_step"], 1)
                v.wait_ge(S0["lambda_step"], 5)
                nc.vector.tensor_tensor(lam_mean[:, 2:3], lam_mean[:, 1:2], lam_mean[:, 0:1],
                                        ALU.subtract).then_inc(S0["lambda_step"], 1)
                v.wait_ge(S0["lambda_step"], 6)
                nc.vector.tensor_scalar(lam_mean[:, 3:4], lam_mean[:, 2:3], 2.0 / HEADS, -LAMBDA_INIT,
                                        ALU.mult, ALU.add).then_inc(S0["lambda_step"], 1)

            @block.scalar
            def _(a):
                a.wait_ge(S0["lambda_step"], 4)
                nc.scalar.activation(lam_exp[:, :, :], lam_sum[:, :, :], ACT.Exp).then_inc(S0["lambda_exp"], 1)

        def write_parts(sp, kind, w, part, first, last, signal):
            for src, dst, order in ((q_part, q_rows, Q_PARTS), (k_part, k_rows, K_PARTS)):
                blocks = [i for i in range(len(order)) if order[i] == part]
                step = blocks[1] - blocks[0] if len(blocks) > 1 else 1
                sp.dma_start(dst[2 * kind + w, blocks[0]:blocks[-1] + 1:step, first:last, :]
                             .rearrange("b r t -> r b t"),
                             src[first:last, part, :].unsqueeze(1)
                             .broadcast_to([last - first, len(blocks), T])).then_inc(signal, 16)

        def project_stage(kind, w, clears, first_seq=None):
            s = SPROJ
            x, v_aug = xs[w], v_augs[w]
            causal_kind = kind == 0
            bq = next_cols[:, BQ:BQ + 1] if causal_kind else tcols[:, T_BQ:T_BQ + 1]
            bk = next_cols[:, BK:BK + 1] if causal_kind else tcols[:, T_BK:T_BK + 1]
            bv = next_rows[:, BV, :] if causal_kind else trows[:, T_BV, :]
            w_qkv = wi if causal_kind else dwi
            with nc.Block() as block:
                @block.sync
                def _(sp):
                    if causal_kind:
                        sp.dma_start(xs[X][:, :, :], x_in[first_seq]).then_inc(SL["x"], 16)
                    if causal_kind:
                        for dst, src in ((next_cols, layer_cols), (wi, layer_wi), (next_rows, layer_rows)):
                            sp.dma_start(dst[:], src[0]).then_inc(s["loaded"], 16)
                        sp.dma_start(xs[Y][:, :, :], x_in[first_seq + 1]).then_inc(SL["y"], 16)
                        sp.wait_ge(SL["y"], 16)
                    for part in range(3):
                        sp.wait_ge(s[("part1", "part2", "part3")[part]], 4)
                        write_parts(sp, kind, w, part, 0, EARLY, s["written"])
                    clear(sp, clears)

                @block.vector
                def _(v):
                    if causal_kind:
                        v.wait_ge(SL["x"], 16)
                        layer_norm_vector(v, s, x, xhat)
                    if causal_kind:
                        v.wait_ge(s["loaded"], 16 * 3)
                    for h in range(2):
                        v.wait_ge(s["qk"], 2 * h + 1)
                        nc.vector.tensor_scalar(q32[:, h * HALF:(h + 1) * HALF], bank(2 + h), bq, SCALE,
                                                ALU.add, ALU.mult).then_inc(s["q32"], 1)
                    n = 0
                    for h in range(2):
                        hs = slice(h * HALF, (h + 1) * HALF)
                        for i, (full, part) in enumerate(((q32, q_part), (k32, k_part))):
                            v.wait_ge(s["part1"], 2 * h + i + 1)
                            nc.vector.tensor_tensor(full[:, hs], full[:, hs], part[:, 0, hs],
                                                    ALU.subtract).then_inc(s["rest"], 1)
                    for h in range(2):
                        hs = slice(h * HALF, (h + 1) * HALF)
                        for i, (full, part) in enumerate(((q32, q_part), (k32, k_part))):
                            v.wait_ge(s["part2"], 2 * h + i + 1)
                            nc.vector.tensor_tensor(part[:, 2, hs], full[:, hs], part[:, 1, hs],
                                                    ALU.subtract).then_inc(s["part3"], 1)
                    for t in range(QT):
                        v.wait_ge(s["v"], 4 * (t // 4 + 1))
                        nc.vector.tensor_tensor(v_aug[:, t, :, 0:HD],
                                                bank(6 + t // 4)[:, (t % 4) * P:(t % 4 + 1) * P]
                                                .rearrange("p (h d) -> p h d", h=HEADS),
                                                bv.rearrange("p (h d) -> p h d", h=HEADS),
                                                ALU.add).then_inc(s["v_ready"], 1)

                @block.gpsimd
                def _(g):
                    if causal_kind:
                        layer_norm_pool(g, s)

                @block.tensor
                def _(pe):
                    if causal_kind:
                        turn_tensor(pe, s["xhat"], s["turned"], xhat, 0)
                    else:
                        turn_tensor(pe, None, s["turned"], x, 0)
                    if causal_kind:
                        pe.wait_ge(s["loaded"], 16 * 3)
                    for h in range(2):
                        pe.wait_ge(s["xnT"], h + 1)
                        for o in range(2):
                            nc.tensor.matmul(bank(2 + 2 * o + h), w_qkv[:, o * D:(o + 1) * D],
                                             xnT[:, h * HALF:(h + 1) * HALF],
                                             start=True, stop=True).then_inc(s["qk"], 1)
                    for t in range(QT):
                        nc.tensor.matmul(bank(6 + t // 4)[:, (t % 4) * P:(t % 4 + 1) * P],
                                         xnT[:, t * P:(t + 1) * P], w_qkv[:, 2 * D:3 * D],
                                         start=True, stop=True).then_inc(s["v"], 1)

                @block.scalar
                def _(a):
                    if causal_kind:
                        a.wait_ge(s["loaded"], 16 * 3)
                    for h in range(2):
                        a.wait_ge(s["turned"], 4 * (h + 1))
                        hs = slice(h * HALF, (h + 1) * HALF)
                        if causal_kind:
                            nc.scalar.activation(xnT[:, hs], bank(h), ACT.Identity, bias=next_cols[:, LN1_B:LN1_B + 1],
                                                 scale=next_cols[:, LN1_W:LN1_W + 1]).then_inc(s["xnT"], 1)
                        else:
                            nc.scalar.activation(xnT[:, hs], bank(h), ACT.Identity).then_inc(s["xnT"], 1)
                    for h in range(2):
                        hs = slice(h * HALF, (h + 1) * HALF)
                        a.wait_ge(s["qk"], 2 * h + 2)
                        nc.scalar.activation(k32[:, hs], bank(4 + h), ACT.Identity, bias=bk).then_inc(s["k32"], 1)
                        a.wait_ge(s["q32"], h + 1)
                        nc.scalar.activation(q_part[:, 0, hs], q32[:, hs], ACT.Identity).then_inc(s["part1"], 1)
                        a.wait_ge(s["k32"], h + 1)
                        nc.scalar.activation(k_part[:, 0, hs], k32[:, hs], ACT.Identity).then_inc(s["part1"], 1)
                    for h in range(2):
                        hs = slice(h * HALF, (h + 1) * HALF)
                        for i, (full, part) in enumerate(((q32, q_part), (k32, k_part))):
                            a.wait_ge(s["rest"], 2 * h + i + 1)
                            nc.scalar.activation(part[:, 1, hs], full[:, hs], ACT.Identity).then_inc(s["part2"], 1)

        def side_entries(entries, item, tick, pace):
            table = {}
            for name, items, ticks in entries:
                table[name] = (int(np.ceil(tick)), item)
                item += items
                tick += ticks * pace if items else ticks
            return table, item, tick

        NORM_TICKS = 15
        SIDE_BANK = 7
        FFN_STEPS = ([(("turn", h), 1, 1) for h in range(2)] + [(("proj", h), 1, 1) for h in range(2)]
                     + [("norm", 0, NORM_TICKS)] + [(("turn_norm", h), 1, 1.5) for h in range(2)]
                     + [(("hidden", n), 1, 1) for n in range(2 * FT)]
                     + [("gap", 0, 0), (("ffn2", 0), 1, 2), ("gap2", 0, 4), (("ffn2", 1), 1, 2)])
        RESIDUAL_STEPS = [("norm", 0, NORM_TICKS + 4), ("sum", 0, 5), ("norm2", 0, NORM_TICKS + 4)]
        PROJECT_STEPS = ([("norm", 0, NORM_TICKS)] + [(("turn", h), 1, 1.5) for h in range(2)]
                         + [((o, h), 1, 1) for h in range(2) for o in ("q", "k")]
                         + [(("v", h), 1, 1) for h in range(2)] + [("split", 0, 4), ("end", 0, 3)])

        PROJECT_LOADS = ((wi, layer_wi), (next_cols, layer_cols), (next_rows, layer_rows))
        FFN_LOADS = ((cols, layer_cols), (rows, layer_rows), (wo, layer_wo), (f1, layer_f1), (f2, layer_f2))

        def side_norm(v, s, src, dst, norms, tick):
            for t in range(QT):
                if t % 2 == 0:
                    yield tick + t // 2
                nc.vector.bn_stats(stats[:, t, :], src[:, t, :]).then_inc(s["stats"], 1)
            yield tick + 4
            v.wait_ge(s["stats"], QT * (norms + 1))
            for t in range(QT):
                nc.vector.bn_aggr(mv[:, t, :], stats[:, t, :]).then_inc(s["moments"], 1)
            v.wait_ge(s["moments"], QT * (norms + 1))
            nc.vector.tensor_scalar(var_eps[:, :], mv[:, :, 1], EPS, None, ALU.add).then_inc(s["var"], 1)
            for t in range(QT):
                if t % 2 == 0:
                    yield tick + NORM_TICKS - 3 + t // 2
                if t == 0:
                    v.wait_ge(s["rstd"], norms + 1)
                nc.vector.tensor_scalar(dst[:, t, :], src[:, t, :], mv[:, t, 0:1], rstd[:, t:t + 1],
                                        ALU.subtract, ALU.mult).then_inc(s["xhat"], 1)

        def side_norm_pool(g, s, norms, tick):
            yield tick + 5
            g.wait_ge(s["var"], norms + 1)
            nc.gpsimd.tensor_tensor(rstd[:, :], var_eps[:, :], neg_half[:, :], ALU.pow).then_inc(s["rstd"], 1)

        class Side:

            def __init__(self, w, ffn, project, start, pace, load=None, prefetch=None, residual=None, parts_free=None):
                self.residual = residual
                self.w, self.ffn, self.project, self.load, self.prefetch = w, ffn, project, load, prefetch
                self.parts_free = parts_free
                item, tick = 0, start
                if ffn:
                    self.F, item, tick = side_entries(FFN_STEPS, item, tick, pace)
                if residual is not None:
                    self.R, item, tick = side_entries(RESIDUAL_STEPS, item, tick, pace)
                if project:
                    self.J, item, tick = side_entries(PROJECT_STEPS, item, tick, pace)
                self.items, self.end = item, tick

            def sync(self, sp):
                s = SIDE[self.w]
                if self.load is not None:
                    yield 0
                    for dst, src in PROJECT_LOADS:
                        sp.dma_start(dst[:], src[self.load]).then_inc(s["loaded"], 16)
                if self.project:
                    for part in range(3):
                        yield (self.J["v", 1][0], self.J["end"][0], self.J["end"][0] + 3)[part]
                        sp.wait_ge(s[("part1", "part2", "part3")[part]], 4)
                        write_parts(sp, 0, self.w, part, 0, D, s["written"])
                    sp.wait_ge(s["written"], 16 * 6)
                if self.residual is not None:
                    yield self.F["proj", 0][0] + 1
                    sp.wait_ge(s["free"], 2)
                    sp.dma_start(attns[self.w][:, :, :], x_in[self.residual]).then_inc(s["x0"], 16)
                if self.prefetch is not None:
                    yield float("inf")
                    sp.wait_ge(s["free"], self.items)
                    for dst, src in FFN_LOADS:
                        sp.dma_start(dst[:], src[self.prefetch]).then_inc(s["prefetched"], 16)
                    sp.wait_ge(s["prefetched"], 16 * len(FFN_LOADS))

            def tensor(self, pe):
                s, w = SIDE[self.w], self.w
                dst = bank(SIDE_BANK)

                def due(step):
                    if step[1]:
                        pe.wait_ge(s["free"], step[1])

                def turn(src, h):
                    for t in range(4 * h, 4 * h + 4):
                        mm = nc.tensor.transpose(dst[:, token_rows(t)], src[:, t, :], ident[:, :])
                    mm.then_inc(s["full"], 1)

                if self.ffn:
                    for h in range(2):
                        yield self.F["turn", h][0]
                        due(self.F["turn", h])
                        turn(attns[w], h)
                    for h in range(2):
                        yield self.F["proj", h][0]
                        due(self.F["proj", h])
                        for t in range(4 * h, 4 * h + 4):
                            mm = nc.tensor.matmul(dst[:, token_rows(t)], xnT[:, t * P:(t + 1) * P], wo[:, :],
                                                  start=True, stop=True)
                        mm.then_inc(s["full"], 1)
                    for h in range(2):
                        yield self.F["turn_norm", h][0]
                        due(self.F["turn_norm", h])
                        pe.wait_ge(s["xhat"], 4 * (h + 1))
                        turn(xhat, h)
                    for n in range(2 * FT):
                        h, f = n // FT, n % FT
                        yield self.F["hidden", n][0]
                        due(self.F["hidden", n])
                        nc.tensor.matmul(dst, f1[:, f * P:(f + 1) * P], xnT[:, h * HALF:(h + 1) * HALF],
                                         start=True, stop=True).then_inc(s["full"], 1)
                    for h in range(2):
                        yield self.F["ffn2", h][0]
                        due(self.F["ffn2", h])
                        pe.wait_ge(s["gelu"], h + 1)
                        for t in range(4 * h, 4 * h + 4):
                            if t % 2 == 0 and t % 4:
                                yield self.F["ffn2", h][0] + 1
                            for f in range(FT):
                                mm = nc.tensor.matmul(dst[:, token_rows(t)], hidA[:, f, t * P:(t + 1) * P],
                                                      f2[:, f, :], start=f == 0, stop=f == FT - 1)
                        mm.then_inc(s["full"], 1)
                if self.project:
                    for h in range(2):
                        yield self.J["turn", h][0]
                        due(self.J["turn", h])
                        pe.wait_ge(s["xhat"], QT * self.ffn + 4 * (h + 1))
                        turn(xhat, h)
                    if self.load is not None:
                        pe.wait_ge(s["loaded"], 16 * len(PROJECT_LOADS))
                    for h in range(2):
                        for o, name in enumerate("qk"):
                            yield self.J[name, h][0]
                            due(self.J[name, h])
                            nc.tensor.matmul(dst, wi[:, o * D:(o + 1) * D], xnT[:, h * HALF:(h + 1) * HALF],
                                             start=True, stop=True).then_inc(s["full"], 1)
                    for h in range(2):
                        yield self.J["v", h][0]
                        due(self.J["v", h])
                        for t in range(4 * h, 4 * h + 4):
                            mm = nc.tensor.matmul(dst[:, token_rows(t)], xnT[:, t * P:(t + 1) * P],
                                                  wi[:, 2 * D:3 * D], start=True, stop=True)
                        mm.then_inc(s["full"], 1)

            def scalar(self, a):
                s = SIDE[self.w]
                src = bank(SIDE_BANK)

                def copy(dst, step, scale=1.0, bias=0.0):
                    a.wait_ge(s["full"], step[1] + 1)
                    nc.scalar.activation(dst, src, ACT.Identity, bias=bias, scale=scale).then_inc(s["free"], 1)

                if self.ffn:
                    for h in range(2):
                        yield self.F["turn", h][0] + 0.5
                        copy(xnT[:, h * HALF:(h + 1) * HALF], self.F["turn", h])
                    for h in range(2):
                        yield self.F["turn_norm", h][0] + 0.5
                        copy(xnT[:, h * HALF:(h + 1) * HALF], self.F["turn_norm", h],
                             cols[:, LN2_W:LN2_W + 1], cols[:, LN2_B:LN2_B + 1])
                    for h in range(2):
                        hs = slice(h * HALF, (h + 1) * HALF)
                        for f in range(FT):
                            last = self.F["hidden", FT * h + f]
                            yield last[0] + 0.5
                            copy(hidA[:, f, hs], last, bias=cols[:, B1 + f:B1 + f + 1])
                        yield last[0] + 1.5
                        a.wait_ge(s["free"], last[1] + 1)
                        nc.scalar.activation(hidA[:, :, hs], hidA[:, :, hs], ACT.Gelu).then_inc(s["gelu"], 1)
                if self.project:
                    if self.load is not None:
                        a.wait_ge(s["loaded"], 16 * len(PROJECT_LOADS))
                    for h in range(2):
                        yield self.J["turn", h][0] + 0.5
                        copy(xnT[:, h * HALF:(h + 1) * HALF], self.J["turn", h],
                             next_cols[:, LN1_W:LN1_W + 1], next_cols[:, LN1_B:LN1_B + 1])
                    for h in range(2):
                        hs = slice(h * HALF, (h + 1) * HALF)
                        yield self.J["k", h][0] + 0.5
                        copy(k32[:, hs], self.J["k", h], bias=next_cols[:, BK:BK + 1])
                        if h == 0 and self.parts_free:
                            a.wait_ge(*self.parts_free)
                        a.wait_ge(s["free"], self.J["k", h][1] + 1)
                        for full_, part in ((q32, q_part), (k32, k_part)):
                            nc.scalar.activation(part[:, 0, hs], full_[:, hs], ACT.Identity).then_inc(s["part1"], 1)
                            yield self.J["k", h][0] + 1
                    for h in range(2):
                        hs = slice(h * HALF, (h + 1) * HALF)
                        for i, (full_, part) in enumerate(((q32, q_part), (k32, k_part))):
                            yield self.J["v", 1][0] + 1 + 2 * h + i
                            a.wait_ge(s["rest"], 2 * h + i + 1)
                            nc.scalar.activation(part[:, 1, hs], full_[:, hs], ACT.Identity).then_inc(s["part2"], 1)

            def gpsimd(self, g):
                s, x = SIDE[self.w], xs[self.w]
                if self.ffn:
                    yield 0
                    nc.gpsimd.tensor_tensor(xb[:, :, :], x[:, :, :], over_tiles(rows[:, BO, :], QT), ALU.add)\
                        .then_inc(s["bias"], 1)
                    yield from side_norm_pool(g, s, 0, self.F["norm"][0])
                    g.wait_ge(s["free"], self.F["proj", 1][1] + 1)
                    nc.gpsimd.tensor_tensor(xb[:, :, :], x[:, :, :], over_tiles(rows[:, B2, :], QT), ALU.add)\
                        .then_inc(s["bias2"], 1)
                if self.residual is not None:
                    yield from side_norm_pool(g, s, 1, self.R["norm"][0])
                    g.wait_ge(s["x0"], 16)
                    nc.gpsimd.tensor_tensor(xb[:, :, :], attns[self.w][:, :, :],
                                            over_tiles(trows[:, FIN_B, :], QT), ALU.add).then_inc(s["sum"], 1)
                    yield from side_norm_pool(g, s, 2, self.R["norm2"][0])
                if self.project:
                    yield from side_norm_pool(g, s, int(self.ffn), self.J["norm"][0])

            def vector(self, v):
                s, x, v_aug = SIDE[self.w], xs[self.w], v_augs[self.w]
                src = bank(SIDE_BANK)

                def add_up(step, h, ready):
                    v.wait_ge(s[ready], 1)
                    v.wait_ge(s["full"], step[1] + 1)
                    nc.vector.tensor_tensor(x[:, 4 * h:4 * h + 4, :], xb[:, 4 * h:4 * h + 4, :],
                                            tokens(src), ALU.add).then_inc(s["free"], 1)

                if self.ffn:
                    for h in range(2):
                        yield self.F["proj", h][0] + 0.5
                        add_up(self.F["proj", h], h, "bias")
                    v.wait_ge(s["free"], self.F["proj", 1][1] + 1)
                    yield from side_norm(v, s, x, xhat, 0, self.F["norm"][0])
                    for h in range(2):
                        yield self.F["ffn2", h][0] + 1.5
                        add_up(self.F["ffn2", h], h, "bias2")
                    v.wait_ge(s["free"], self.F["ffn2", 1][1] + 1)
                if self.residual is not None:
                    yield from side_norm(v, s, x, xhat, 1, self.R["norm"][0])
                    yield self.R["sum"][0]
                    v.wait_ge(s["xhat"], 2 * QT)
                    nc.vector.tensor_tensor(xhat[:, :, :], xhat[:, :, :], over_tiles(trows[:, FIN_W, :], QT),
                                            ALU.mult).then_inc(s["scaled"], 1)
                    yield self.R["sum"][0] + 2
                    v.wait_ge(s["scaled"], 1)
                    v.wait_ge(s["sum"], 1)
                    nc.vector.tensor_tensor(x[:, :, :], xhat[:, :, :], xb[:, :, :], ALU.add).then_inc(s["scaled"], 1)
                    v.wait_ge(s["scaled"], 2)
                    yield from side_norm(v, s, x, x, 2, self.R["norm2"][0])
                if self.project:
                    yield from side_norm(v, s, x, xhat, int(self.ffn), self.J["norm"][0])
                    if self.load is not None:
                        v.wait_ge(s["loaded"], 16 * len(PROJECT_LOADS))
                    for h in range(2):
                        yield self.J["q", h][0] + 0.5
                        v.wait_ge(s["full"], self.J["q", h][1] + 1)
                        nc.vector.tensor_scalar(q32[:, h * HALF:(h + 1) * HALF], src, next_cols[:, BQ:BQ + 1], SCALE,
                                                ALU.add, ALU.mult).then_inc(s["free"], 1)
                    def value_rows(h):
                        v.wait_ge(s["full"], self.J["v", h][1] + 1)
                        nc.vector.tensor_tensor(
                            v_aug[:, 4 * h:4 * h + 4, :, 0:HD],
                            tokens(src).rearrange("p t (h d) -> p t h d", h=HEADS),
                            next_rows[:, BV, :].rearrange("p (h d) -> p h d", h=HEADS).unsqueeze(1)
                            .broadcast_to([P, 4, HEADS, HD]), ALU.add).then_inc(s["free"], 1)

                    def rest(h, i):
                        full_, part, hs = (q32, k32)[i], (q_part, k_part)[i], slice(h * HALF, (h + 1) * HALF)
                        v.wait_ge(s["part1"], 2 * h + i + 1)
                        nc.vector.tensor_tensor(full_[:, hs], full_[:, hs], part[:, 0, hs],
                                                ALU.subtract).then_inc(s["rest"], 1)

                    first, last = self.J["v", 0][0], self.J["v", 1][0]
                    yield first
                    rest(0, 0)
                    yield first + 1
                    value_rows(0)
                    rest(0, 1)
                    yield last + 1
                    value_rows(1)
                    yield last + 2
                    rest(1, 0)
                    yield last + 3
                    rest(1, 1)
                    for h in range(2):
                        hs = slice(h * HALF, (h + 1) * HALF)
                        for i, (full_, part) in enumerate(((q32, q_part), (k32, k_part))):
                            yield last + 4 + 2 * h + i
                            v.wait_ge(s["part2"], 2 * h + i + 1)
                            nc.vector.tensor_tensor(part[:, 2, hs], full_[:, hs], part[:, 1, hs],
                                                    ALU.subtract).then_inc(s["part3"], 1)

        def beside(generator):
            pending = [0]

            def run(tick):
                while pending[0] is not None and pending[0] <= tick:
                    pending[0] = next(generator, None)
            return run

        def attention_stage(kind, w, clears, fresh=False, side=None, head=False, tail=False):
            s, attn = SATT[w], attns[w]
            H = int(head)
            full = kind == 1
            HALF_TILES = (QT, QT if full else QT // 2)
            NC = sum(HALF_TILES)
            NS = 2 * NC
            NG = NC // 2
            DIAG = [] if full else [4, 5, 6, 7, 8, 9, 10, 11]
            MT1, MT0, OT0, OT1 = 9, 3, 4, 12 if full else 11
            m_loaded, s_loaded, max_sent = ((s["m_loaded0"], s["m_loaded1"]), (s["s_loaded0"], s["s_loaded1"]),
                                            (s["max_rows0"], s["max_rows1"]))

            def loads(u, par):
                return 32 * u + 64 - 32 * par - (64 * H if par == 0 else 0)

            def loads_one(u, par):
                return 32 * u + 64 - 32 * par - 64 * H

            def sent(pairs, half):
                return 32 * (pairs - H * half)

            def sequence(u):
                return w if u < PAIRS else 1 - w

            def chunk(c):
                half, j = (1, c) if c < QT else (0, c - QT)
                return half, j, 0 if full else max(0, (j - 4 * half) * P)

            def score(i):
                if i < 16:
                    half, r, h, kb = 1, i // 4, (i // 2) % 2, i % 2
                elif full:
                    half, r, h, kb = 0, (i - 16) // 4, (i // 2) % 2, i % 2
                else:
                    half, r, h, kb = 0, (i - 16) // 2, i % 2, 0
                return half, r, h, kb, (r + 1) * P if (not full and kb == half) else 4 * P

            def flags(where):
                cur = where in ("first", "inner", "last")
                nxt = where in ("before", "first", "inner")
                prev = where in ("inner", "last", "after")
                return cur, nxt, prev

            RING = 3
            RING_BANKS = (0, 1, 2)
            ST_RING = 3
            OT_TILES = 4 if full else 2

            def ring_items(where):
                cur, nxt, prev = flags(where)
                place, slots_ = 0, []
                for c in range(NC):
                    items = []
                    if nxt:
                        items += [("score", 2 * c), ("score", 2 * c + 1)]
                    if cur and c == MT0:
                        items.append(("max0", 0))
                    if nxt and c == MT1:
                        items.append(("max1", 0))
                    if prev and c == OT0:
                        items += [("out0", t) for t in range(0, 4, OT_TILES)]
                    if cur and c == OT1:
                        items += [("out1", t) for t in range(0, 4, OT_TILES)]
                    slots_.append([(what, i, place + n) for n, (what, i) in enumerate(items)])
                    place += len(items)
                return slots_

            def uses(where):
                return sum(len(items) for items in ring_items(where))

            def place_of(where, what, i=0):
                return [p for items in ring_items(where) for w, j, p in items if (w, j) == (what, i)][0]

            WHERE = ("before", "first") + ("inner",) * (PAIRS - 2) + ("inner" if tail else "last", "after")

            def ring_base(u):
                return sum(uses(WHERE[i]) for i in range(H, u + 1))

            def tick_of(u):
                return (u + 1 - H) * NC

            def ring_bank(item):
                return bank(RING_BANKS[item % RING])

            def chunk_bank(item):
                return bank(3 + item % ST_RING)

            def walk(step):
                for u in range(H - 1, PAIRS + 1):
                    step(u, u % 2, WHERE[u + 1])

            def no_side(tick):
                pass

            with nc.Block() as block:
                @block.sync
                def _(sp):

                    def head_rows(rows_, head_):
                        first = head_ % HEADS * HD
                        return rows_[2 * kind + sequence(head_ // 2), :, first:first + HD, :]

                    def load_queries(dst, u, par, signal):
                        for h in range(2):
                            sp.dma_start(dst[HROWS * h:HROWS * (h + 1), par, h, :], head_rows(q_rows, 2 * u + h))\
                                .then_inc(signal, 16)

                    def load_keys(dst, u, par, signal):
                        for h in range(2):
                            sp.dma_start(dst[HROWS * h:HROWS * (h + 1), par, :], head_rows(k_rows, 2 * u + h))\
                                .then_inc(signal, 16)

                    def load_pass_one(u, par, wait):
                        if wait:
                            sp.wait_ge(s["max_ready"], 2 * (u - 1 - H))
                        load_queries(QM, u, par, m_loaded[par])
                        load_keys(KM, u, par, m_loaded[par])

                    def load_pass_two(u, par, wait):
                        if wait:
                            sp.wait_ge(s["exp_done"], (u - 1) * 2 * NC)
                        load_queries(QS, u, par, s_loaded[par])
                        load_keys(KS, u, par, s_loaded[par])

                    def max_rows(u, par, half):
                        step_, what = (u, "max0") if half == 0 else (u - 1, "max1")
                        sp.wait_ge(s["ring_free"], ring_base(step_) + place_of(WHERE[step_ + 1], what) + 1)
                        if u >= H:
                            sp.wait_ge(s_loaded[par], loads(u, par))
                        for h in range(2):
                            r = HROWS * h + MAX_ROW
                            sp.dma_start(QS[r:r + 2, par, h, half * HALF:(half + 1) * HALF],
                                         maxT[8 * h:8 * h + 8, half, :]).then_inc(max_sent[half], 16)

                    run_side = beside(side.sync(sp)) if side else no_side
                    if fresh and kind == 0:
                        sp.wait_ge(SLATE["written"], 16 * 8)
                    if fresh:
                        sp.wait_ge(SPROJ["written"], 16 * 6)
                    if not head:
                        load_pass_one(0, 0, False)
                    if fresh:
                        for part in range(3):
                            write_parts(sp, kind, w, part, EARLY, D, SPROJ["written_rest"])
                    if not head:
                        load_pass_two(0, 0, False)
                        load_pass_one(1, 1, False)
                    clear(sp, clears)
                    run_side(0)
                    if not head:
                        max_rows(0, 0, 1)
                    if fresh:
                        sp.wait_ge(SPROJ["written_rest"], 16 * 6)
                    for u in range(PAIRS):
                        tick = tick_of(u)
                        if u + 1 < PAIRS + tail:
                            load_pass_two(u + 1, (u + 1) % 2, u > 0)
                        if u + 2 < PAIRS:
                            load_pass_one(u + 2, u % 2, u + 2 - 1 - H > 0)
                        run_side(tick + 1)
                        max_rows(u, u % 2, 0)
                        run_side(tick + MT0 + 1)
                        if tail and u + 1 == PAIRS:
                            load_pass_one(PAIRS + 1, 1, True)
                            run_side(float("inf"))
                        if tail and u + 2 == PAIRS:
                            run_side(10 ** 6)
                            load_pass_one(PAIRS, 0, True)
                        if u + 1 < PAIRS + tail:
                            max_rows(u + 1, (u + 1) % 2, 1)
                        run_side(tick + MT1 + 1)
                    if tail:
                        sp.wait_ge(m_loaded[1], loads_one(PAIRS + 1, 1))
                    run_side(float("inf"))
                    if fresh and kind == 0:
                        sp.wait_ge(SLATE["loaded"], 16 * len(LATE))
                    for half in range(2):
                        sp.wait_ge(max_sent[half], sent(PAIRS + (half if tail else 0), half))

                @block.gpsimd
                def _(g):

                    def stage_values(u, par, wait):
                        if wait:
                            g.wait_ge(s["pv_done"], (u - 1) * NG)
                        if u == PAIRS:
                            g.wait_ge(SIDE[1 - w]["free"], side.J["v", 1][1] + 1)
                        h = 2 * u % HEADS
                        nc.gpsimd.tensor_copy(v_pair[:, par], v_augs[sequence(u)][:, :, h:h + 2, :])\
                            .then_inc(s["v_staged"], 1)

                    def split_max(w, half):
                        i = 2 * w + (1 - half)
                        g.wait_ge(s["max_found"], i + 1 - 2 * H)
                        nm = neg_max[:, half].rearrange("p t h -> p h t")
                        nc.gpsimd.tensor_copy(max_bf[:, half, :, 0, :], nm).then_inc(s["max_step"], 1)
                        g.wait_ge(s["max_step"], i + 1 - 2 * H)
                        nc.gpsimd.tensor_tensor(max_bf[:, half, :, 1, :], nm, max_bf[:, half, :, 0, :],
                                                ALU.subtract).then_inc(s["max_ready"], 1)

                    def normalise(w, half, step_, where):
                        e = 2 * w + (1 - half)
                        place = place_of(where, "out0" if half == 0 else "out1", 4 - OT_TILES)
                        g.wait_ge(s["ring_free"], ring_base(step_) + place + 1)
                        nc.gpsimd.tensor_tensor(o_sum[:, half], o_turned[:, half, :, :, 0], o_turned[:, half, :, :, 1],
                                                ALU.add).then_inc(s["o_step"], 1)
                        g.wait_ge(s["o_step"], 2 * e + 1)
                        nc.gpsimd.tensor_tensor(o_rec[:, half], o_sum[:, half, :, :, HD], minus_one[:, :, :],
                                                ALU.pow).then_inc(s["o_step"], 1)
                        g.wait_ge(s["o_step"], 2 * e + 2)
                        nc.gpsimd.tensor_tensor(
                            attn[:, 4 * half:4 * half + 4, bass.ds(2 * HD * w, 2 * HD)]
                            .rearrange("p t (h d) -> p t h d", h=2),
                            o_sum[:, half, :, :, 0:HD],
                            o_rec[:, half].unsqueeze(3).broadcast_to([P, 4, 2, HD]), ALU.mult)\
                            .then_inc(s["normed"], 1)

                    run_side = beside(side.gpsimd(g)) if side else no_side

                    def step(u, par, where):
                        cur, nxt, prev = flags(where)
                        tick = tick_of(u)
                        if nxt:
                            stage_values(u + 1, 1 - par, prev)
                        run_side(tick + 1)
                        if prev and where != "after":
                            normalise(u - 1, 0, u, where)
                        run_side(tick + OT0 + 1)
                        if nxt:
                            split_max(u + 1, 1)
                        run_side(tick + QT)
                        if nxt:
                            split_max(u + 1, 0)
                        if cur:
                            normalise(u, 1, u, where)
                        run_side(tick + NC)
                    walk(step)
                    run_side(float("inf"))

                @block.tensor
                def _(pe):
                    run_side = beside(side.tensor(pe)) if side else no_side

                    def step(u, par, where):
                        cur, nxt, prev = flags(where)
                        base = ring_base(u)

                        def ring(place):
                            if base + place >= RING:
                                pe.wait_ge(s["ring_free"], base + place - RING + 1)
                            return ring_bank(base + place)

                        def values(v, vpar, i):
                            half, j, _ = chunk(2 * i)
                            first, last = j == 0, j + 2 == HALF_TILES[1 - half]
                            pe.wait_ge(s["exp_done"], 2 * (v * NC + 2 * i + 2))
                            if first and half == 1:
                                if v + 1 - H > 0:
                                    pe.wait_ge(s["v_staged"], v + 1 - H)
                                if v > 0:
                                    pe.wait_ge(s["o_evac"], 2 * v)
                            if first and half == 0:
                                pe.wait_ge(s["o_evac"], 2 * v + 1)
                            for h in range(2):
                                if first and not full and half == 0:
                                    nc.tensor.matmul(bank(6)[64 * h + 32:64 * h + 32 + HD + 1, 0:P],
                                                     v_pair[:, vpar, 1, h, :], zeros[:, :], start=True, stop=False,
                                                     skip_group_check=True)
                            for odd in range(2):
                                _, jj, c0 = chunk(2 * i + odd)
                                for h in range(2):
                                    r = 64 * h + 32 * odd
                                    mm = nc.tensor.matmul(
                                        bank(6)[r:r + HD + 1, c0:HALF], v_pair[:, vpar, jj, h, :],
                                        probs[:, (2 * i + odd) % 4, h, c0:HALF],
                                        start=first and c0 == 0, stop=last, skip_group_check=True)
                            mm.then_inc(s["pv_done"], 1)

                        def turn_out(v, half, tile, place):
                            e = 2 * v + (1 - half)
                            dst = ring(place)
                            pe.wait_ge(s["o_evac"], e + 1)
                            for t in range(tile, tile + OT_TILES):
                                mm = nc.tensor.transpose(dst[:, t * P:(t + 1) * P],
                                                         o_sb[:, 1 - half, t * P:(t + 1) * P], ident[:, :])
                            mm.then_inc(s["ring_full"], 1)

                        def turn_max(v, half, place):
                            dst = ring(place)
                            if v >= H:
                                pe.wait_ge(s["max_ready"], 2 * (v - H) + (1 - half) + 1)
                            nc.tensor.transpose(dst[0:16, 0:P // 2].bitcast(BF16),
                                                max_bf[:, half].rearrange("p h l t -> p (h l t)"),
                                                identb[:, :]).then_inc(s["ring_full"], 1)

                        for c, items in enumerate(ring_items(where)):
                            def scores(i, place):
                                half, r, h, kb, n = score(i)
                                if i == 0:
                                    if loads_one(u + 1, 1 - par) > 0:
                                        pe.wait_ge(m_loaded[1 - par], loads_one(u + 1, 1 - par))
                                dst = ring(place)
                                qt = 4 * half + r
                                nc.tensor.matmul(dst[:, 0:n], QM[:, 1 - par, h, qt * P:(qt + 1) * P],
                                                 KM[:, 1 - par, kb * HALF:kb * HALF + n],
                                                 start=True, stop=True).then_inc(s["ring_full"], 1)

                            def chunk_scores(h):
                                half, j, c0 = chunk(c)
                                if h == 0 and (c == 0 or c == QT):
                                    if u >= H:
                                        pe.wait_ge(s_loaded[par], loads(u, par))
                                    if sent(u + 1, half) > 0:
                                        pe.wait_ge(max_sent[half], sent(u + 1, half))
                                item = 2 * (u * NC + c) + h
                                if item >= ST_RING:
                                    pe.wait_ge(s["exp_done"], item - ST_RING + 1)
                                dst = chunk_bank(item)
                                mm = nc.tensor.matmul(dst[:, c0:HALF], KS[:, par, j * P:(j + 1) * P],
                                                      QS[:, par, h, half * HALF + c0:(half + 1) * HALF],
                                                      start=True, stop=c not in DIAG)
                                if c in DIAG:
                                    mm = nc.tensor.matmul(dst[:, c0:c0 + P], identb[:, :], later[:, :],
                                                          start=False, stop=True)
                                mm.then_inc(s["st_full"], 1)

                            for what, i, place in items:
                                if what == "score" and i % 2 == 0:
                                    scores(i, place)
                            if cur:
                                chunk_scores(0)
                            for what, i, place in items:
                                if what == "score" and i % 2 == 1:
                                    scores(i, place)
                            if cur:
                                chunk_scores(1)
                            for what, i, place in items:
                                if what == "max0":
                                    turn_max(u, 0, place)
                                if what == "max1":
                                    turn_max(u + 1, 1, place)
                            if prev and c == 1:
                                values(u - 1, 1 - par, NG - 1)
                            if cur and c >= 3 and c % 2 == 1:
                                values(u, par, (c - 3) // 2)
                            for what, i, place in items:
                                if what == "out0":
                                    turn_out(u - 1, 0, i, place)
                                if what == "out1":
                                    turn_out(u, 1, i, place)
                            run_side(tick_of(u) + c)
                    walk(step)
                    run_side(float("inf"))

                @block.scalar
                def _(a):

                    def evacuate(v, half, groups, wait):
                        e = 2 * v + (1 - half)
                        a.wait_ge(s["pv_done"], groups)
                        if wait:
                            a.wait_ge(s["normed"], e - 1)
                        nc.scalar.activation(o_sb[:, 1 - half, :], bank(6), ACT.Identity).then_inc(s["o_evac"], 1)

                    run_side = beside(side.scalar(a)) if side else no_side

                    def step(u, par, where):
                        cur, nxt, prev = flags(where)
                        for c in range(NC):
                            run_side(tick_of(u) + c)
                            if cur:
                                half, j, c0 = chunk(c)
                                if u > 0 or c >= 4:
                                    a.wait_ge(s["pv_done"], u * NG + c // 2 - 1)
                                for h in range(2):
                                    item = 2 * (u * NC + c) + h
                                    a.wait_ge(s["st_full"], item + 1)
                                    nc.scalar.activation(probs[:, c % 4, h, c0:HALF], chunk_bank(item)[:, c0:HALF],
                                                         ACT.Exp).then_inc(s["exp_done"], 1)
                            if prev and c == 1:
                                evacuate(u - 1, 0, u * NG, True)
                            if cur and c == 9:
                                evacuate(u, 1, u * NG + 4, u > 0)
                    walk(step)
                    run_side(float("inf"))

                @block.vector
                def _(v):

                    run_side = beside(side.vector(v)) if side else no_side

                    def step(u, par, where):
                        base = ring_base(u)

                        def full_bank(place):
                            v.wait_ge(s["ring_full"], base + place + 1)
                            return ring_bank(base + place)

                        def find_max(half, place):
                            v.wait_ge(s["ring_free"], base + place + 1)
                            nb = 2 if full or half == 1 else 1
                            nc.vector.tensor_reduce(neg_max[:, half], parts[:, half, :, :, 0:nb], op=ALU.max,
                                                    axis=AX.X, negate=True).then_inc(s["max_found"], 1)

                        def copy_max(pair, half, place):
                            src = full_bank(place)
                            if sent(pair, half) > 0:
                                v.wait_ge(max_sent[half], sent(pair, half))
                            nc.vector.tensor_copy(maxT[:, half, :], src[0:16, 0:P // 2].bitcast(BF16))\
                                .then_inc(s["ring_free"], 1)

                        def copy_out(w, half, tile, place):
                            src = full_bank(place).rearrange("p (t h g c) -> p t h g c", t=4, h=2, g=2)
                            if w > 0:
                                v.wait_ge(s["normed"], 2 * w - half)
                            ts = slice(tile, tile + OT_TILES)
                            nc.vector.tensor_copy(o_turned[:, half, ts].rearrange("p t h g c -> p t (h g) c"),
                                                  src[:, ts, :, :, 0:HD + 1].rearrange("p t h g c -> p t (h g) c"))\
                                .then_inc(s["ring_free"], 1)

                        def last_normalise(place):
                            v.wait_ge(s["ring_free"], base + place + 1)
                            nc.vector.tensor_tensor(o_sum[:, 0], o_turned[:, 0, :, :, 0], o_turned[:, 0, :, :, 1],
                                                    ALU.add).then_inc(s["last_step"], 1)
                            v.wait_ge(s["last_step"], 1)
                            nc.vector.reciprocal(o_rec[:, 0], o_sum[:, 0, :, :, HD]).then_inc(s["last_step"], 1)
                            v.wait_ge(s["last_step"], 2)
                            nc.vector.tensor_tensor(
                                attn[:, 0:4, D - 2 * HD:D].rearrange("p t (h d) -> p t h d", h=2),
                                o_sum[:, 0, :, :, 0:HD],
                                o_rec[:, 0].unsqueeze(3).broadcast_to([P, 4, 2, HD]), ALU.mult)\
                                .then_inc(s["normed"], 1)

                        for c, items in enumerate(ring_items(where)):
                            run_side(tick_of(u) + c)
                            for what, i, place in items:
                                if what == "score":
                                    half, r, h, kb, n = score(i)
                                    dst = parts[:, half, r, h, kb:kb + 1]
                                    if full or kb != half:
                                        src = full_bank(place)
                                        nc.vector.tensor_reduce(dst, src, op=ALU.max, axis=AX.X)\
                                            .then_inc(s["ring_free"], 1)
                                    else:
                                        src = full_bank(place)
                                        nc.vector.tensor_tensor_reduce(
                                            out=masked_out[:, i % 4, 0:n], in0=src[:, 0:n],
                                            in1=causal[:, 4 * P - n:4 * P], scale=1.0, scalar=LOWEST,
                                            op0=ALU.add, op1=ALU.max, accum_out=dst).then_inc(s["ring_free"], 1)
                                    if i == 15:
                                        find_max(1, place)
                                    if i == NS - 1:
                                        find_max(0, place)
                                if what == "max0":
                                    copy_max(u, 0, place)
                                if what == "max1":
                                    copy_max(u + 1, 1, place)
                                if what == "out0":
                                    copy_out(u - 1, 0, i, place)
                                if what == "out1":
                                    copy_out(u, 1, i, place)
                                if what == "out0" and where == "after" and i == 4 - OT_TILES:
                                    last_normalise(place)
                    walk(step)
                    run_side(float("inf"))

        def turned_half(a, turned, signal, dst, b0, h, scale=1.0, bias=0.0):
            a.wait_ge(turned, 4 * (h + 1))
            nc.scalar.activation(dst[:, h * HALF:(h + 1) * HALF], bank(b0 + h), ACT.Identity, bias=bias,
                                 scale=scale).then_inc(signal, 1)

        def token_rows(t):
            return slice((t % 4) * P, (t % 4 + 1) * P)

        def tokens(b_):
            return b_.rearrange("p (t d) -> p t d", t=4)

        def over_tiles(row, n):
            return row.unsqueeze(1).broadcast_to([P, n, row.shape[-1]])

        def output_projection(s, w, w_out, bias_row):
            x, attn = xs[w], attns[w]

            def tensor(pe):
                turn_tensor(pe, None, s["attn_turned"], attn, 0)
                for t in range(QT):
                    if t % 4 == 0:
                        pe.wait_ge(s["attnT"], t // 4 + 1)
                    nc.tensor.matmul(bank(2 + t // 4)[:, token_rows(t)], xnT[:, t * P:(t + 1) * P], w_out[:, :],
                                     start=True, stop=True).then_inc(s["proj"], 1)

            def scalar(a):
                for h in range(2):
                    turned_half(a, s["attn_turned"], s["attnT"], xnT, 0, h)

            def gpsimd(g):
                nc.gpsimd.tensor_tensor(xb[:, :, :], x[:, :, :], over_tiles(bias_row, QT), ALU.add)\
                    .then_inc(s["bias"], 1)

            def vector(v):
                v.wait_ge(s["bias"], 1)
                for h in range(2):
                    v.wait_ge(s["proj"], 4 * (h + 1))
                    nc.vector.tensor_tensor(x[:, 4 * h:4 * h + 4, :], xb[:, 4 * h:4 * h + 4, :],
                                            tokens(bank(2 + h)), ALU.add).then_inc(s["resid"], 1)
                v.wait_ge(s["resid"], 2)
            return tensor, scalar, gpsimd, vector

        def ternary_stage(w, clears):
            x = xs[w]
            s = ST

            def hidden_layer(pe, w, src, signal, ready):
                pe.wait_ge(ready, 2 * FT)
                for n in range(2 * FT):
                    h, f = n // FT, n % FT
                    for i in range(FT):
                        mm = nc.tensor.matmul(bank(n), w[:, i, f * P:(f + 1) * P], src[:, i, h * HALF:(h + 1) * HALF],
                                              start=i == 0, stop=i == FT - 1)
                    mm.then_inc(signal, 1)

            with nc.Block() as block:
                @block.sync
                def _(sp):
                    clear(sp, clears)

                @block.gpsimd
                def _(g):
                    layer_norm_pool(g, s)

                @block.tensor
                def _(pe):
                    turn_tensor(pe, None, s["turned"], x, 0)
                    for n in range(2 * FT):
                        h, f = n // FT, n % FT
                        pe.wait_ge(s["xnT"], h + 1)
                        if n >= 3:
                            pe.wait_ge(s["hidden"], n - 2)
                        for i, (w, signal) in enumerate(((tw1, s["gate"]), (tw2, s["up"]))):
                            nc.tensor.matmul(bank(2 + 2 * (n % 3) + i), w[:, f * P:(f + 1) * P],
                                             xnT[:, h * HALF:(h + 1) * HALF], start=True, stop=True)\
                                .then_inc(signal, 1)
                    hidden_layer(pe, th1, hidB, s["h1"], s["hidden"])
                    hidden_layer(pe, th2, hidA, s["h2"], s["g1"])
                    pe.wait_ge(s["g2"], 2 * FT)
                    for t in range(QT):
                        for f in range(FT):
                            mm = nc.tensor.matmul(bank(t // 4)[:, token_rows(t)], hidB[:, f, t * P:(t + 1) * P],
                                                  tw3[:, f, :], start=f == 0, stop=f == FT - 1)
                        mm.then_inc(s["w3"], 1)

                @block.scalar
                def _(a):
                    for h in range(2):
                        turned_half(a, s["turned"], s["xnT"], xnT, 0, h)
                    for n in range(2 * FT):
                        h, f = n // FT, n % FT
                        a.wait_ge(s["gate"], n + 1)
                        nc.scalar.activation(hidA[:, f, h * HALF:(h + 1) * HALF], bank(2 + 2 * (n % 3)), ACT.Silu,
                                             scale=tcols[:, S_W1 + f:S_W1 + f + 1]).then_inc(s["silu"], 1)
                    for ready, signal, dst, col in ((s["h1"], s["g1"], hidA, S_H1), (s["h2"], s["g2"], hidB, S_H2)):
                        for n in range(2 * FT):
                            h, f = n // FT, n % FT
                            a.wait_ge(ready, n + 1)
                            nc.scalar.activation(dst[:, f, h * HALF:(h + 1) * HALF], bank(n), ACT.Gelu,
                                                 scale=tcols[:, col + f:col + f + 1]).then_inc(signal, 1)

                @block.vector
                def _(v):
                    for n in range(2 * FT):
                        h, f = n // FT, n % FT
                        v.wait_ge(s["up"], n + 1)
                        v.wait_ge(s["silu"], n + 1)
                        hs = slice(h * HALF, (h + 1) * HALF)
                        nc.vector.scalar_tensor_tensor(out=hidB[:, f, hs], in0=bank(3 + 2 * (n % 3)),
                                                       scalar=tcols[:, S_W2 + f:S_W2 + f + 1], in1=hidA[:, f, hs],
                                                       op0=ALU.mult, op1=ALU.mult).then_inc(s["hidden"], 1)
                    for h in range(2):
                        v.wait_ge(s["w3"], 4 * (h + 1))
                        nc.vector.tensor_tensor(xb[:, 4 * h:4 * h + 4, :], tokens(bank(h)),
                                                over_tiles(trows[:, S_W3, :], 4), ALU.mult).then_inc(s["scaled"], 1)
                    v.wait_ge(s["scaled"], 2)
                    nc.vector.tensor_tensor(x[:, :, :], x[:, :, :], xb[:, :, :], ALU.add).then_inc(s["sum"], 1)
                    v.wait_ge(s["sum"], 1)
                    layer_norm_vector(v, s, x, x)

        def differential_stage(w, clears):
            s, x, attn = SF, xs[w], attns[w]
            proj_tensor, proj_scalar, proj_gpsimd, proj_vector = output_projection(s, w, dwo, trows[:, T_BP, :])
            with nc.Block() as block:
                @block.sync
                def _(sp):
                    clear(sp, clears)

                @block.gpsimd
                def _(g):
                    proj_gpsimd(g)
                    layer_norm_pool(g, s)

                @block.vector
                def _(v):
                    nc.vector.scalar_tensor_tensor(out=attn[:, :, 0:D // 2], in0=attn[:, :, D // 2:D],
                                                   scalar=lam_mean[:, 3:4], in1=attn[:, :, 0:D // 2],
                                                   op0=ALU.mult, op1=ALU.add).then_inc(s["mixed"], 1)
                    proj_vector(v)
                    layer_norm_vector(v, s, x, x)

                @block.scalar
                def _(a):
                    proj_scalar(a)

                @block.tensor
                def _(pe):
                    pe.wait_ge(s["mixed"], 1)
                    proj_tensor(pe)

        def experts_stage(seq, w, clears):
            s, x = SM, xs[w]
            loaded = (s["loaded0"], s["loaded1"])
            with nc.Block() as block:
                @block.sync
                def _(sp):
                    clear(sp, clears)

                    def load(e, par, wait):
                        if wait:
                            wait_alone(sp, s["y"], 2 * (e - 1))
                        sp.dma_start(ew1[:, par, :], moe_w1[e]).then_inc(loaded[par], 16)
                        sp.dma_start(ew2[:, par, :, :], moe_w2[e]).then_inc(loaded[par], 16)
                    load(0, 0, False)
                    load(1, 1, False)
                    with sp.Fori(2, EXPERTS - 1, 2) as e:
                        load(e, 0, True)
                        load(e + 1, 1, True)
                    if w == Y:
                        for i in range(2):
                            sp.wait_ge(s["xhat"], QT * (i + 1))
                            sp.dma_start(out[seq - 1 + i], xs[i][:, :, :]).then_inc(s["stored"], 16)
                            sp.wait_ge(s["stored"], 16 * (i + 1))

                @block.gpsimd
                def _(g):
                    if w == Y:
                        for i in range(2):
                            g.wait_ge(s["var"], i + 1)
                            nc.gpsimd.tensor_tensor(rstd[:, :], var_eps[:, :], neg_half[:, :], ALU.pow)\
                                .then_inc(s["rstd"], 1)

                @block.tensor
                def _(pe):
                    turn_tensor(pe, None, s["turned"], x, 0)
                    pe.wait_ge(s["xnT"], 2)
                    for t in range(QT):
                        mm = nc.tensor.matmul(bank(1)[:, t * EXPERTS:(t + 1) * EXPERTS], xnT[:, t * P:(t + 1) * P],
                                              sw[:, :], start=True, stop=True)
                    mm.then_inc(s["logits"], 1)

                    def expert(e, par, first, second=False):
                        hid = (hidA, hidB)[par]
                        pe.wait_ge(loaded[par], 16 * e + 32 - 16 * par)
                        for n in range(2 * FT):
                            h, f = n // FT, n % FT
                            if not first or n >= 4:
                                pe.wait_ge(s["gelu"], 2 * FT * e + n - 3)
                            nc.tensor.matmul(bank(2 + n % 4), ew1[:, par, f * P:(f + 1) * P],
                                             xnT[:, h * HALF:(h + 1) * HALF], start=True, stop=True)\
                                .then_inc(s["hidden"], 1)
                        for h in range(2):
                            pe.wait_ge(s["gelu"], 2 * FT * e + FT * (h + 1))
                            if not first:
                                pe.wait_ge(s["tmp"], 2 * e - 1 + h)
                            for t in range(4 * h, 4 * h + 4):
                                for f in range(FT):
                                    mm = nc.tensor.matmul(bank(6 + h)[:, token_rows(t)], hid[:, f, t * P:(t + 1) * P],
                                                          ew2[:, par, f, :], start=f == 0, stop=f == FT - 1)
                            mm.then_inc(s["y"], 1)
                    expert(0, 0, True)
                    expert(1, 1, False)
                    with pe.Fori(2, EXPERTS - 1, 2) as e:
                        expert(e, 0, False)
                        expert(e + 1, 1, False)

                @block.scalar
                def _(a):
                    for h in range(2):
                        turned_half(a, s["turned"], s["xnT"], xnT, 0, h)
                    a.wait_ge(s["step"], 3)
                    nc.scalar.activation(lexp[:, :, :], logit[:, :, :], ACT.Exp).then_inc(s["lexp"], 1)

                    def expert(e, par, wait):
                        hid = (hidA, hidB)[par]
                        for n in range(2 * FT):
                            h, f = n // FT, n % FT
                            if wait and n == 0:
                                wait_alone(a, s["y"], 2 * e - 2)
                            wait_alone(a, s["hidden"], 2 * FT * e + n + 1)
                            nc.scalar.activation(hid[:, f, h * HALF:(h + 1) * HALF], bank(2 + n % 4),
                                                 ACT.Gelu_apprx_tanh, bias=eb1[:, e, f:f + 1]).then_inc(s["gelu"], 1)
                    expert(0, 0, False)
                    expert(1, 1, False)
                    with a.Fori(2, EXPERTS - 1, 2) as e:
                        expert(e, 0, True)
                        expert(e + 1, 1, True)

                @block.vector
                def _(v):
                    step = [0]

                    def then(ins):
                        step[0] += 1
                        ins.then_inc(s["step"], 1)
                        v.wait_ge(s["step"], step[0])

                    def per_token(a_):
                        return a_.unsqueeze(2).broadcast_to([P, QT, EXPERTS])

                    if w == Y:
                        layer_norm_vector(v, s, xs[X], xs[X])
                    v.wait_ge(s["logits"], 1)
                    logits = bank(1)[:, 0:QT * EXPERTS].rearrange("p (t e) -> p t e", e=EXPERTS)
                    then(nc.vector.tensor_tensor(logit[:, :, :], logits, over_tiles(swb[:, :], QT), ALU.add))
                    then(nc.vector.tensor_reduce(lmax[:, :], logit[:, :, :], op=ALU.max, axis=AX.X))
                    then(nc.vector.tensor_tensor(logit[:, :, :], logit[:, :, :], per_token(lmax[:, :]), ALU.subtract))
                    v.wait_ge(s["lexp"], 1)
                    then(nc.vector.tensor_reduce(lsum[:, :], lexp[:, :, :], op=ALU.add, axis=AX.X))
                    then(nc.vector.reciprocal(lsum[:, :], lsum[:, :]))
                    then(nc.vector.tensor_tensor(prob[:, :, :], lexp[:, :, :], per_token(lsum[:, :]), ALU.mult))
                    then(nc.vector.tensor_reduce(lmax[:, :], prob[:, :, :], op=ALU.max, axis=AX.X))
                    then(nc.vector.tensor_tensor(gate[:, :, :], prob[:, :, :], per_token(lmax[:, :]), ALU.is_equal))
                    then(nc.vector.tensor_tensor(gate[:, :, :], gate[:, :, :], over_tiles(rank[:, :], QT), ALU.mult))
                    then(nc.vector.tensor_reduce(lsum[:, :], gate[:, :, :], op=ALU.max, axis=AX.X))
                    then(nc.vector.tensor_tensor(gate[:, :, :], gate[:, :, :], per_token(lsum[:, :]), ALU.is_equal))
                    then(nc.vector.tensor_tensor(gate[:, :, :], gate[:, :, :], per_token(lmax[:, :]), ALU.mult))

                    def expert(e, first):
                        for h in range(2):
                            v.wait_ge(s["y"], 2 * e + h + 1)
                            if not first:
                                v.wait_ge(s["acc"], QT * e - 4 + 4 * h)
                            nc.vector.tensor_tensor(xhat[:, 4 * h:4 * h + 4, :], tokens(bank(6 + h)),
                                                    over_tiles(eb2[:, e, :], 4), ALU.add).then_inc(s["tmp"], 1)
                            v.wait_ge(s["tmp"], 2 * e + h + 1)
                            for t in range(4 * h, 4 * h + 4):
                                nc.vector.scalar_tensor_tensor(out=x[:, t, :], in0=xhat[:, t, :],
                                                               scalar=gate[:, t, bass.ds(e, 1)], in1=x[:, t, :],
                                                               op0=ALU.mult, op1=ALU.add).then_inc(s["acc"], 1)
                    expert(0, True)
                    with v.Fori(1, EXPERTS) as e:
                        expert(e, False)
                    v.wait_ge(s["acc"], QT * EXPERTS)
                    if w == Y:
                        layer_norm_vector(v, s, x, x, norms=1)

        with nc.Fori(0, B - 1, 2) as b:
            project_stage(0, X, [S0, SM], b)
            attention_stage(0, X, [SL], fresh=True, tail=True,
                            side=Side(Y, False, True, 2, 1.5, prefetch=0, parts_free=(SPROJ["written_rest"], 16 * 6)))
            with nc.Fori(0, LAYERS - 1) as l:
                attention_stage(0, Y, [SPROJ, SATT[X], SIDE[Y]], head=True, tail=True,
                                side=Side(X, True, True, 1, 1.0, load=l + 1))
                attention_stage(0, X, [SATT[Y], SIDE[X]], head=True, tail=True,
                                side=Side(Y, True, True, 1, 1.0, prefetch=l + 1))
            attention_stage(0, Y, [SATT[X], SIDE[Y]], head=True, side=Side(X, True, False, 1, 1.5, residual=b))
            ternary_stage(X, [SATT[Y], SIDE[X]])
            project_stage(1, X, [ST])
            attention_stage(1, X, [], fresh=True, side=Side(Y, True, False, 8, 2, residual=b + 1))
            ternary_stage(Y, [SPROJ, SATT[X], SIDE[Y]])
            project_stage(1, Y, [ST])
            attention_stage(1, Y, [], fresh=True)
            differential_stage(X, [SPROJ, SATT[Y]])
            experts_stage(b, X, [SF])
            differential_stage(Y, [SM])
            experts_stage(b + 1, Y, [SF])


def kernel(**inputs):
    import concourse.bacc as bacc
    from concourse.bass_utils import run_bass_kernel_spmd
    import ml_dtypes
    bf16 = np.dtype(ml_dtypes.bfloat16)
    g = {k: np.asarray(v) for k, v in inputs.items()}

    def a(name):
        return g["L0_attn_" + name]

    def columns(v):
        return v.reshape(-1, P).T

    def spread(v):
        return np.broadcast_to(v[None], (P,) + v.shape)

    def tiles(w):
        return w.reshape(-1, P, w.shape[-1]).transpose(1, 0, 2)

    def blocks(rows):
        lead = rows.shape[:-3]
        return np.moveaxis(rows.reshape(lead + (HEADS, -1, HD, T)), -3, -4).reshape(lead + (-1, D, T))

    layer_cols = np.stack([np.concatenate([
        columns(a("ln1_w")[i]), columns(a("ln1_b")[i]), columns(a("ln2_w")[i]), columns(a("ln2_b")[i]),
        columns(a("in_proj_b")[i, 0:D]), columns(a("in_proj_b")[i, D:2 * D]), columns(a("ffn1_b")[i])], 1)
        for i in range(LAYERS)])
    layer_rows = np.stack([spread(np.stack([a("in_proj_b")[i, 2 * D:], a("out_proj_b")[i], a("ffn2_b")[i]]))
                           for i in range(LAYERS)])
    tail_cols = np.concatenate([columns(g["L0_ffn_" + n]) for n in ("w1_s", "w2_s", "h1_s", "h2_s")]
                               + [columns(g["L1_attn_bq"]), columns(g["L1_attn_bk"])], 1)
    tail_rows = spread(np.stack([a("final_w"), a("final_b"), g["L0_ffn_w3_s"], g["L1_attn_bv"], g["L1_attn_bp"]]))
    lambdas = spread(np.stack([g["L1_attn_lambda_" + n][:, 0, :] for n in ("q1", "k1", "q2", "k2")]))

    pos = np.arange(T)
    ident = np.eye(P, dtype=np.float32)
    causal = np.zeros((P, 4 * P), np.float32)
    causal[:, 3 * P:] = np.where(np.arange(P)[None, :] > np.arange(P)[:, None], MASKED, 0.0)
    later = np.where(np.arange(P)[:, None] > np.arange(P)[None, :], MASKED, 0.0).astype(bf16)
    slopes = ((2.0 ** -(2.0 ** -(np.log2(HEADS) - 3))) ** np.arange(1, HEADS + 1)).astype(np.float32)
    q_extra = np.zeros((2, HEADS, EXTRA_ROWS, T), bf16)
    rest = slopes.copy()
    for i in range(3):
        part = rest.astype(bf16)
        q_extra[0, :, 2 * i:2 * i + 2, :] = part[:, None, None]
        rest = rest - part.astype(np.float32)
    k_extra = np.zeros((HEADS, EXTRA_ROWS, T), bf16)
    for i in range(3):
        k_extra[:, 2 * i, :] = (pos // 256 * 256).astype(bf16)
        k_extra[:, 2 * i + 1, :] = (pos % 256).astype(bf16)
    k_extra[:, 6:8, :] = 1.0

    arrays = {
        "x": g["L0_attn_x"].reshape(B, QT, P, D).transpose(0, 2, 1, 3),
        "layer_wi": a("in_proj_w").transpose(0, 2, 1),
        "layer_wo": a("out_proj_w").transpose(0, 2, 1),
        "layer_f1": a("ffn1_w").transpose(0, 2, 1),
        "layer_f2": np.stack([tiles(a("ffn2_w")[i].T) for i in range(LAYERS)]),
        "layer_cols": layer_cols, "layer_rows": layer_rows,
        "tern_w1": g["L0_ffn_w1_w"].T, "tern_w2": g["L0_ffn_w2_w"].T,
        "tern_h1": tiles(g["L0_ffn_h1_w"].T), "tern_h2": tiles(g["L0_ffn_h2_w"].T),
        "tern_w3": tiles(g["L0_ffn_w3_w"].T),
        "tail_cols": tail_cols, "tail_rows": tail_rows,
        "diff_w": np.concatenate([g["L1_attn_Wq"].T, g["L1_attn_Wk"].T, g["L1_attn_Wv"].T], 1),
        "diff_wp": g["L1_attn_Wp"].T, "lambdas": lambdas,
        "switch_w": g["L1_ffn_switch_w"], "switch_b": spread(g["L1_ffn_switch_b"]),
        "moe_w1": g["L1_ffn_w1"], "moe_b1": g["L1_ffn_b1"].reshape(EXPERTS, FT, P).transpose(2, 0, 1),
        "moe_w2": np.stack([tiles(g["L1_ffn_w2"][e]) for e in range(EXPERTS)]),
        "moe_b2": spread(g["L1_ffn_b2"]),
        "ident": ident, "identb": ident.astype(bf16), "causal": causal, "later": later,
        "q_extra": blocks(q_extra), "k_extra": blocks(k_extra),
    }
    nc = bacc.Bacc("TRN2", target_bir_lowering=False, num_devices=1)
    args = []
    for name in arrays:
        arrays[name] = np.ascontiguousarray(arrays[name])
        args.append(nc.dram_tensor("in_" + name, arrays[name].shape, mybir.dt.from_np(arrays[name].dtype),
                                   kind="ExternalInput").ap())
    out = nc.dram_tensor("out", (B, P, QT, D), F32, kind="ExternalOutput").ap()
    build(nc, *args, out)
    result = run_bass_kernel_spmd(nc, [{"in_" + k: v for k, v in arrays.items()}], core_ids=[0])
    return result.results[0]["out"].transpose(0, 2, 1, 3).reshape(B, T, D)
```
